# Optimizing a Trainium2 kernel written in Bass

```python
import numpy as np
import jax
import jax.numpy as jnp

def _softmax(x, axis=-1):
    return jax.nn.softmax(x, axis=axis)

def _gelu(x):
    return jax.nn.gelu(x, approximate=True)

def _silu(x):
    return jax.nn.silu(x)

def _sigmoid(x):
    return jax.nn.sigmoid(x)

def _layernorm(x, axis=-1, eps=1e-05):
    m = jnp.mean(x, axis=axis, keepdims=True)
    v = jnp.var(x, axis=axis, keepdims=True)
    return (x - m) / jnp.sqrt(v + eps)

def _scatter_add(tgt, idx, src, axis=0):
    return tgt.at[idx].add(src)

def _segment_sum(src, seg, n):
    return jax.ops.segment_sum(src, seg, n)
kernel_name = 'mk_prb_d1_jaxref_r8_603534'

def setup_inputs(seed: int=0):
    np.random.seed(seed)
    _w = jnp.asarray

    def _L0_attn_setup():
        import jax, jax.numpy as jnp
        import numpy as np
        N_HEAD = 16
        MIN_CTX = 32
        FULL_CTX = 128

        def _pruning_ratio(T):
            if T < MIN_CTX:
                return 1.0
            if T >= FULL_CTX:
                return 0.2
            progress = (T - MIN_CTX) / (FULL_CTX - MIN_CTX)
            return 0.5 - 0.3 * progress
        key = jax.random.key(seed)
        ks = jax.random.split(key, 3)
        B, T, C = (2, 256, 128)
        x = jax.random.normal(ks[0], (B, T, C), jnp.float32)
        w_attn = jax.random.normal(ks[1], (3 * C, C), jnp.float32) * 0.02
        b_attn = jnp.zeros((3 * C,), jnp.float32)
        w_proj = jax.random.normal(ks[2], (C, C), jnp.float32) * 0.02
        b_proj = jnp.zeros((C,), jnp.float32)
        return {'x': x, 'w_attn': w_attn, 'b_attn': b_attn, 'w_proj': w_proj, 'b_proj': b_proj}
    _L0_attn_in = _L0_attn_setup()

    def _L0_ffn_setup():
        import jax, jax.numpy as jnp
        import numpy as np
        B, S, D_MODEL, D_FF, E, R, TOP_K = (4, 256, 128, 512, 8, 16, 2)
        key = jax.random.key(seed)
        ks = jax.random.split(key, 9)
        sd = 1.0 / np.sqrt(D_MODEL)
        return {'hidden_states': jax.random.normal(ks[0], (B, S, D_MODEL), jnp.float32), 'wi': jax.random.normal(ks[1], (D_FF, D_MODEL), jnp.float32) * sd, 'bi': jax.random.normal(ks[2], (D_FF,), jnp.float32) * 0.01, 'wo': jax.random.normal(ks[3], (D_MODEL, D_FF), jnp.float32) * (1.0 / np.sqrt(D_FF)), 'bo': jax.random.normal(ks[4], (D_MODEL,), jnp.float32) * 0.01, 'lora_A': jax.random.normal(ks[5], (E, R, D_MODEL), jnp.float32) * sd, 'lora_B': jax.random.normal(ks[6], (E, D_FF, R), jnp.float32) * 0.02, 'gate_w': jax.random.normal(ks[7], (E, D_MODEL), jnp.float32) * sd, 'gate_b': jax.random.normal(ks[8], (E,), jnp.float32) * 0.01}
    _L0_ffn_in = _L0_ffn_setup()
    _d = {'L0_attn_x': _L0_attn_in['x'], 'L0_attn_w_attn': _L0_attn_in['w_attn'], 'L0_attn_b_attn': _L0_attn_in['b_attn'], 'L0_attn_w_proj': _L0_attn_in['w_proj'], 'L0_attn_b_proj': _L0_attn_in['b_proj'], 'L0_ffn_wi': _L0_ffn_in['wi'], 'L0_ffn_bi': _L0_ffn_in['bi'], 'L0_ffn_wo': _L0_ffn_in['wo'], 'L0_ffn_bo': _L0_ffn_in['bo'], 'L0_ffn_lora_A': _L0_ffn_in['lora_A'], 'L0_ffn_lora_B': _L0_ffn_in['lora_B'], 'L0_ffn_gate_w': _L0_ffn_in['gate_w'], 'L0_ffn_gate_b': _L0_ffn_in['gate_b']}
    _x0 = _d['L0_attn_x']
    _d['L0_attn_x'] = jax.random.normal(jax.random.fold_in(jax.random.key(seed), 1), (8, 512, 128), dtype=_x0.dtype)
    del _x0
    return _d

def reference(L0_attn_x, L0_attn_w_attn, L0_attn_b_attn, L0_attn_w_proj, L0_attn_b_proj, L0_ffn_wi, L0_ffn_bi, L0_ffn_wo, L0_ffn_bo, L0_ffn_lora_A, L0_ffn_lora_B, L0_ffn_gate_w, L0_ffn_gate_b):

    def _L0_attn_ref(x, w_attn, b_attn, w_proj, b_proj):
        import jax, jax.numpy as jnp
        import numpy as np
        N_HEAD = 16
        MIN_CTX = 32
        FULL_CTX = 128

        def _pruning_ratio(T):
            if T < MIN_CTX:
                return 1.0
            if T >= FULL_CTX:
                return 0.2
            progress = (T - MIN_CTX) / (FULL_CTX - MIN_CTX)
            return 0.5 - 0.3 * progress
        B, T, C = x.shape
        nh = N_HEAD
        hd = C // nh
        neg_inf = jnp.float32(-jnp.inf)
        qkv = x @ w_attn.T + b_attn
        q, k, v = jnp.split(qkv, 3, axis=2)
        to_heads = lambda t: t.reshape(B, T, nh, hd).transpose(0, 2, 1, 3)
        q, k, v = (to_heads(q), to_heads(k), to_heads(v))
        att = jnp.einsum('bhid,bhjd->bhij', q, k) / jnp.sqrt(jnp.float32(hd))
        i = jnp.arange(T)
        causal = i[None, :] <= i[:, None]
        att = jnp.where(causal[None, None], att, neg_inf)
        S = jax.nn.relu(att[:, 0])
        S = S.at[..., 0].set(0.0)
        S = S * (1.0 - jnp.eye(T, dtype=S.dtype))
        S_shifted = jnp.concatenate([jnp.zeros((B, 1, T), S.dtype), S[:, :-1]], axis=1)
        FF = jnp.cumsum(S_shifted, axis=1)
        att = att - FF[:, None]
        ratio = _pruning_ratio(T)
        memory_budget = max(1, int(T * ratio))
        if ratio < 1.0:
            FF_mod = jnp.where(causal[None], FF, jnp.inf)
            sorted_idx = jnp.argsort(FF_mod, axis=-1)
            rank = jnp.argsort(sorted_idx, axis=-1)
            eff_k = jnp.minimum(memory_budget - 1, i + 1)
            keep = rank < eff_k[None, :, None]
            keep = keep | jnp.eye(T, dtype=bool)[None]
            att = jnp.where(keep[:, None], att, neg_inf)
        y = jax.nn.softmax(att, axis=-1) @ v
        y = y.transpose(0, 2, 1, 3).reshape(B, T, C)
        return y @ w_proj.T + b_proj

    def _L0_ffn_ref(hidden_states, wi, bi, wo, bo, lora_A, lora_B, gate_w, gate_b):
        import jax, jax.numpy as jnp
        import numpy as np
        B, S, D_MODEL, D_FF, E, R, TOP_K = (4, 256, 128, 512, 8, 16, 2)
        logits = jnp.einsum('bsd,ed->bse', hidden_states, gate_w) + gate_b
        scores = jax.nn.softmax(logits, axis=-1)
        top_v, top_i = jax.lax.top_k(scores, TOP_K)
        val_sum = top_v.sum(axis=-1)
        out = jnp.zeros_like(hidden_states)
        for e in range(E):
            count = (top_i == e).sum(axis=-1).astype(hidden_states.dtype)
            gate = count * val_sum
            inter = jnp.einsum('bsd,fd->bsf', hidden_states, wi) + bi + jnp.einsum('bsr,fr->bsf', jnp.einsum('bsd,rd->bsr', hidden_states, lora_A[e]), lora_B[e])
            h = jax.nn.relu(inter)
            expert_out = jnp.einsum('bsf,df->bsd', h, wo) + bo
            out = out + gate[..., None] * expert_out
        return out
    x = L0_attn_x
    xn = _layernorm(x, axis=-1)
    x = x + _L0_attn_ref(xn, L0_attn_w_attn, L0_attn_b_attn, L0_attn_w_proj, L0_attn_b_proj) + _L0_ffn_ref(xn, L0_ffn_wi, L0_ffn_bi, L0_ffn_wo, L0_ffn_bo, L0_ffn_lora_A, L0_ffn_lora_B, L0_ffn_gate_w, L0_ffn_gate_b)
    return x

_drawn_inputs = setup_inputs


def setup_inputs(seed=0):
    import zlib

    import numpy as np

    out = dict(_drawn_inputs(seed))
    spreads = {'L0_attn_b_attn': (0.0, 0.531), 'L0_attn_b_proj': (0.0, 0.1)}
    factors = {'L0_attn_w_attn': 8.0,
     'L0_attn_w_proj': 3.586,
     'L0_ffn_bi': 8.0,
     'L0_ffn_bo': 6.371,
     'L0_ffn_gate_b': 23.412}
    for name, (base, spread) in spreads.items():
        noise = np.random.default_rng([zlib.crc32(name.encode()), seed]).standard_normal(out[name].shape)
        drawn = base * np.exp(spread * noise) if base else spread * noise
        out[name] = jnp.asarray(drawn.astype(out[name].dtype))
    for name, factor in factors.items():
        out[name] = (out[name] * factor).astype(out[name].dtype)
    return out
```

```python
from contextlib import ExitStack

import concourse.bass as bass
from concourse import mybir

F32 = mybir.dt.float32
BF16 = mybir.dt.bfloat16
ALU = mybir.AluOpType
ACT = mybir.ActivationFunctionType
AX = mybir.AxisListType.X

P = 128
B, T, C = 8, 512, 128
NH, HD = 16, 8
NA = T // P
FF, NE, R = 512, 8, 16
NF = FF // P
KEEP = max(1, int(T * 0.2)) - 1
SCALE = 1.0 / HD ** 0.5
EPS = 1e-5
BIG = 1.0e30
MARK = -3.0e38
PAD = -KEEP % 8
ROUNDS = (KEEP + PAD) // 8
VW = HD + 1

Q_PART = (0, 0, 1, 1, 0, 2)
K_PART = (0, 1, 0, 1, 2, 0)
STACK = 8 * len(Q_PART)

UNITS = [(a, h, 4 // w) for a, w in ((0, 1), (1, 2), (2, 4), (3, 4)) for h in range(0, NH, 4 // w)]
NU = len(UNITS)
LAST = [max(u for u in range(NU) if UNITS[u][0] == a) for a in range(NA)]
HEADS_TO = [sum(x[2] for x in UNITS[:u + 1]) for u in range(NU)]
OFF = [P * a * (a + 1) // 2 for a in range(NA + 1)]
WOFF = [OFF[a] + PAD * a for a in range(NA + 1)]
FOFF = [sum(T - P * x for x in range(c)) for c in range(NA + 1)]

NA_RING, NP_RING = 4, 3
TAIL = 10

FFN_JOBS = [("z", 1, "act"), ("mask0", 3, "dve"), ("mask1", 5, "dve")] + \
    [(f"h{f}{s}", 10 + 3 * (2 * f + s), "act") for f in range(NF) for s in range(2)] + \
    [("down", 36, "dve")]
ATT_JOBS = [(f"yt{a}", LAST[a] + 7, "act") for a in range(NA)] + \
    [("proj0", 38, "dve"), ("proj1", LAST[3] + 9, "dve")]
PREP_JOBS = [("xt", 4, "act"), ("q", 6, "act"), ("k", 7, "act"), ("v", 8, "dve"), ("gate", 9, "dve")] + \
    [(f"s{c}", 15 + c, "dve") for c in range(NA)] + [(f"f{a}", 20 + a, "act") for a in range(NA)]
SETUP_JOBS = ["w_attn", "w_in", "w_out", "lora_b", "small", "rows"]


class Plan:

    def __init__(self, steps, preps, setup):
        jobs = [(-1, (name, 0), "act") for name in SETUP_JOBS] if setup else []
        for k in range(steps):
            jobs += [(NU * k + o, (name, k), who) for name, o, who in FFN_JOBS + ATT_JOBS]
        for n in range(preps):
            jobs += [(NU * n + o, (name, n), who) for name, o, who in PREP_JOBS]
        jobs.sort(key=lambda x: x[0])
        self.at, self.number, self.order, self.reads = {}, {}, [], {}
        counts = {"act": 0, "dve": 0}
        for i, (t, key, who) in enumerate(jobs):
            self.at.setdefault(t, []).append(key)
            self.number[key] = i
            self.order.append(key)
            counts[who] += 1
            self.reads[key] = (who, counts[who])


def build(nc, x, w_attn, b_attn, w_proj, b_proj, wi, bi, wo, bo, lora_a, lora_b, gate_w, gate_b, out):
    ctx = ExitStack()
    with ctx:
        def sb(name, shape, dt=F32):
            return ctx.enter_context(nc.sbuf_tensor(name, shape, dt))

        def sem(name):
            return ctx.enter_context(nc.semaphore(name))

        ident = sb("ident", [P, P])
        ident16 = sb("ident16", [P, P], BF16)
        ones = sb("ones", [P, T])
        later = sb("later", [P, 2, T])
        causal = sb("causal", [P, P])
        minus_half = sb("minus_half", [P, NA])
        rank = sb("rank", [P, NA, NE])
        raw = sb("raw", [P, 3 * P + 4 * P + 4 * P + 4 * P + P + P])
        raw_attn = raw[:, 0:384].rearrange("p (t c) -> p t c", t=3)
        raw_wi = raw[:, 384:896].rearrange("p (f c) -> p f c", f=NF)
        raw_wo = raw[:, 896:1408]
        raw_b = raw[:, 1408:1920].rearrange("p (f e r) -> p f e r", f=NF, e=NE)
        raw_a = raw[:, 1920:2048]
        raw_wp = raw[:, 2048:2176]
        raw_gate = sb("raw_gate", [NE, C])
        raw_bi = sb("raw_bi", [NF, P])
        raw_bqk = sb("raw_bqk", [2, P])
        bqk_dh = sb("bqk_dh", [2, P])
        bias_row = sb("bias_row", [1, P + NE])
        bp_row = sb("bp_row", [1, C])
        bo_row = sb("bo_row", [1, C])
        bo2_row = sb("bo2_row", [1, C])
        wq = sb("wq", [C, P])
        wk = sb("wk", [C, P])
        wv = sb("wv", [C, P])
        wi_t = sb("wi_t", [C, FF])
        wo_t = sb("wo_t", [P, NF, C])
        b_t = sb("b_t", [NE * R, FF])
        a_t = sb("a_t", [C, NE * R])
        wp_t = sb("wp_t", [P, C])
        gate_t = sb("gate_t", [C, NE])
        bi_col = sb("bi_col", [P, NF])
        bqk_col = sb("bqk_col", [P, 2])
        bias_b = sb("bias_b", [P, P + NE])
        xs = sb("xs", [P, 2, NA, C])
        stats = sb("stats", [P, NA, 6])
        mv = sb("mv", [P, NA, 2])
        var = sb("var", [P, NA])
        rstd = sb("rstd", [P, NA])
        xn = sb("xn", [P, NA, C])
        xnt = sb("xnt", [C, 2, T])
        qk32 = sb("qk32", [P, 2, T])
        parts = sb("parts", [P, 2, 3, T], BF16)
        rest = sb("rest", [P, T])
        qs = sb("qs", [STACK, 2, NH, T], BF16)
        ks = sb("ks", [STACK, 2, NH, T], BF16)
        va = sb("va", [P, 2, NA, NH * VW])
        s0 = sb("s0", [P, FOFF[NA]])
        ft = sb("ft", [P, FOFF[NA]])
        nf = sb("nf", [P, WOFF[NA]])
        wk_sel = sb("wk_sel", [P, WOFF[NA]])
        top8 = sb("top8", [P, NA, 8])
        mask = sb("mask", [P, 2, OFF[NA]])
        logit = sb("logit", [P, NA, NE])
        less = sb("less", [P, NA, NE + 1])
        expd = sb("expd", [P, NA, NE + 1])
        eq = sb("eq", [P, NA, NE])
        tie = sb("tie", [P, NA, NE])
        hot = sb("hot", [P, 2, NA, NE])
        best = sb("best", [P, 4, NA])
        den = sb("den", [P, NA])
        vsum = sb("vsum", [P, 2, NA])
        hot_x = sb("hot_x", [P, 2, 2, NA, NE * R], BF16)
        z = sb("z", [P, T])
        zm = sb("zm", [P, 2, T])
        h = sb("h", [P, 4, T])
        hsum = sb("hsum", [P, NF, T])
        down = sb("down", [P, NA, C])
        ar = sb("ar", [P, NA_RING, T])
        mx = sb("mx", [P, NA_RING, 4])
        pr = sb("pr", [P, NP_RING, T])
        rec = sb("rec", [P, NH])
        y = sb("y", [P, NA, NH, HD])
        yt = sb("yt", [P, NA, P])
        res = sb("res", [P, NA, C])

        def bank(name):
            return ctx.enter_context(nc.psum_tensor(name, [P, 512], F32))

        ps_s = [bank(f"ps_s{i}") for i in range(2)]
        ps_t = [bank(f"ps_t{i}") for i in range(2)]
        ps_o = bank("ps_o")
        ps_m = [bank(f"ps_m{i}") for i in range(3)]

        names = ["w_in", "x_in", "const", "w_prep", "scored", "masked", "shifted", "turned", "weighed",
                 "summed", "normed", "m_full", "act_read", "dve_read", "varred", "rooted", "xn_done",
                 "split", "stacked", "less_done", "exp_done", "hot_done", "hot_wide", "scanned", "nf_done",
                 "selected", "mask_done", "h_sum", "stored", "dve_chain", "pool_chain",
                 "act_chain", "sel"]
        s = {n: sem(n) for n in names}
        w_in, x_in, const, w_prep = s["w_in"], s["x_in"], s["const"], s["w_prep"]
        scored, masked, shifted, turned = s["scored"], s["masked"], s["shifted"], s["turned"]
        weighed, summed, normed = s["weighed"], s["summed"], s["normed"]
        m_full, act_read, dve_read = s["m_full"], s["act_read"], s["dve_read"]
        varred, rooted, xn_done, split, stacked = s["varred"], s["rooted"], s["xn_done"], s["split"], s["stacked"]
        less_done, exp_done, hot_done, hot_wide = s["less_done"], s["exp_done"], s["hot_done"], s["hot_wide"]
        scanned, nf_done, selected, mask_done = s["scanned"], s["nf_done"], s["selected"], s["mask_done"]
        h_sum, stored = s["h_sum"], s["stored"]
        dve_chain, pool_chain, act_chain, sel = s["dve_chain"], s["pool_chain"], s["act_chain"], s["sel"]

        x_d = x.rearrange("b (a p) c -> b p a c", p=P)
        out_d = out.rearrange("b (a p) c -> b p a c", p=P)

        def run_block(i, steps, preps, setup=False):
            plan = Plan(steps, preps, setup)
            into = (lambda n: 0) if setup else (lambda n: 1 - n)
            end = NU * max(steps, preps) + (TAIL if steps else 0)

            def full(name, k):
                return plan.number[name, k] + 1

            def wait_full(eng, name, k):
                eng.wait_ge(m_full, full(name, k))

            def wait_read(eng, name, k):
                who, n = plan.reads[name, k]
                eng.wait_ge(act_read if who == "act" else dve_read, n)

            def m_bank(name, k):
                return ps_m[plan.number[name, k] % 3]

            with nc.Block() as block:

                def store(sp, k, part):
                    wait_read(sp, ("proj0", "proj1")[part], k)
                    lo, hi = ((0, NA - 1), (NA - 1, NA))[part]
                    b = i * 2 + k
                    sp.dma_start(out_d[bass.ds(b, 1), :, lo:hi, :].rearrange("o p a c -> p (o a) c"),
                                 res[:, lo:hi, :]).then_inc(stored, 16)

                @block.sync
                def _(sp):
                    if setup:
                        sp.dma_start(xs[:, 0, :, :], x_d[0]).then_inc(x_in, 16)
                        sp.dma_start(raw_attn, w_attn.rearrange("(t p) c -> p t c", p=P)).then_inc(w_in, 16)
                        sp.dma_start(raw_wi, wi.rearrange("(f p) c -> p f c", p=P)).then_inc(w_in, 16)
                        sp.dma_start(raw_wo, wo).then_inc(w_in, 16)
                        for f in range(NF):
                            sp.dma_start(raw_b[:, f], lora_b[:, P * f:P * f + P, :].rearrange("e p r -> p e r"))\
                                .then_inc(w_in, 16)
                        sp.dma_start(raw_a, lora_a.rearrange("e r c -> (e r) c")).then_inc(w_in, 16)
                        sp.dma_start(raw_wp, w_proj).then_inc(w_in, 16)
                        sp.dma_start(raw_gate[:, :], gate_w).then_inc(w_in, 16)
                        sp.dma_start(raw_bi[:, :], bi.rearrange("(f p) -> f p", p=P)).then_inc(w_in, 16)
                        sp.dma_start(raw_bqk[:, :], b_attn[0:2 * P].rearrange("(t p) -> t p", p=P)).then_inc(w_in, 16)
                        sp.dma_start(bias_row[:, 0:P], b_attn[2 * P:3 * P].rearrange("(o p) -> o p", o=1))\
                            .then_inc(w_in, 16)
                        sp.dma_start(bias_row[:, P:P + NE], gate_b.rearrange("(o p) -> o p", o=1)).then_inc(w_in, 16)
                        sp.dma_start(bp_row[:, :], b_proj.rearrange("(o p) -> o p", o=1)).then_inc(w_in, 16)
                        sp.dma_start(bo_row[:, :], bo.rearrange("(o p) -> o p", o=1)).then_inc(w_in, 16)
                    for k in range(max(steps, preps)):
                        if k < preps:
                            if not setup:
                                if k >= 1:
                                    wait_read(sp, "down", k - 1)
                                b = i * 2 + (1 + k)
                                sp.dma_start(xs[:, into(k), :, :],
                                             x_d[bass.ds(b, 1)].rearrange("o p a c -> p (o a) c")).then_inc(x_in, 16)
                            for t in range(2):
                                if t == 0 and k >= 1 and not setup:
                                    sp.wait_ge(scored, NU * k)
                                sp.wait_ge(split, 2 * k + t + 1)
                                stack, part = ((qs, Q_PART), (ks, K_PART))[t]
                                for j in range(len(part)):
                                    sp.dma_start(stack[8 * j:8 * j + 8, into(k), :, :], parts[:, t, part[j], :])\
                                        .then_inc(stacked, 16)
                        if k >= 1 and steps:
                            store(sp, k - 1, 1)
                        if k < steps:
                            store(sp, k, 0)
                    if steps:
                        store(sp, steps - 1, 1)
                        sp.wait_ge(stored, 32 * steps)
                    sp.wait_ge(stacked, 192 * preps)

                @block.gpsimd
                def _(pool):
                    chain = [0]

                    def link(ins):
                        chain[0] += 1
                        ins.then_inc(pool_chain, 1)
                        pool.wait_ge(pool_chain, chain[0])

                    if setup:
                        link(nc.gpsimd.memset(ident[:, :], 0.0))
                        nc.gpsimd.affine_select(out=ident[:, :], in_=ident[:, :], compare_op=ALU.not_equal, fill=1.0,
                                                base=0, pattern=[[-1, P]], channel_multiplier=1).then_inc(const, 1)
                        link(nc.gpsimd.memset(minus_half[:, :], -0.5))
                        link(nc.gpsimd.memset(ident16[:, :], 0.0))
                        link(nc.gpsimd.affine_select(out=ident16[:, :], in_=ident16[:, :], compare_op=ALU.not_equal,
                                                     fill=1.0, base=0, pattern=[[-1, P]], channel_multiplier=1))
                        link(nc.gpsimd.memset(later[:, :, :], 1.0))
                        for j in range(2):
                            link(nc.gpsimd.affine_select(out=later[:, j, :], in_=later[:, j, :], compare_op=ALU.is_gt,
                                                         fill=0.0, base=0, pattern=[[1, T]], channel_multiplier=-1))
                        link(nc.gpsimd.affine_select(out=later[:, 0, :], in_=later[:, 0, :], compare_op=ALU.is_gt,
                                                     fill=0.0, base=0, pattern=[[0, T]], channel_multiplier=1))
                        link(nc.gpsimd.memset(causal[:, :], 0.0))
                        link(nc.gpsimd.affine_select(out=causal[:, :], in_=causal[:, :], compare_op=ALU.is_ge,
                                                     fill=-BIG, base=0, pattern=[[-1, P]], channel_multiplier=1))
                        for a in range(NA):
                            link(nc.gpsimd.memset(nf[:, WOFF[a]:WOFF[a] + PAD], BIG))
                        nc.gpsimd.memset(va[:, :, :, :], 1.0).then_inc(const, 1)

                    for t in range(end):
                        k, o = divmod(t, NU)
                        if k < steps:
                            a, h0, g = UNITS[o]
                            w = P * (a + 1)
                            for j in range(g):
                                col = ar[:, t % NA_RING, w * j:w * j + w]
                                pool.wait_ge(masked, NH * NA * k + HEADS_TO[o] - g + j + 1)
                                nc.gpsimd.tensor_scalar(col, col, -1.0, mx[:, t % NA_RING, j:j + 1], ALU.mult, ALU.add)\
                                    .then_inc(shifted, 1)
                        if k < preps and o == 1:
                            pool.wait_ge(varred, k + 1)
                            if setup:
                                pool.wait_ge(pool_chain, chain[0])
                            nc.gpsimd.tensor_tensor(rstd[:, :], var[:, :], minus_half[:, :], ALU.pow).then_inc(rooted, 1)
                        if k < preps and o in (8, 9):
                            j = o - 8
                            wait_read(pool, ("q", "k")[j], k)
                            if k >= 1:
                                pool.wait_ge(stacked, 192 * k)
                            link(nc.gpsimd.tensor_copy(parts[:, j, 0, :], qk32[:, j, :]))
                            link(nc.gpsimd.tensor_tensor(rest[:, :], qk32[:, j, :], parts[:, j, 0, :], ALU.subtract))
                            link(nc.gpsimd.tensor_copy(parts[:, j, 1, :], rest[:, :]))
                            nc.gpsimd.tensor_tensor(parts[:, j, 2, :], rest[:, :], parts[:, j, 1, :], ALU.subtract)\
                                .then_inc(split, 1)
                            pool.wait_ge(split, 2 * k + j + 1)
                        if k < preps and o == 12:
                            pool.wait_ge(hot_done, k + 1)
                            if k >= 1 and not setup:
                                wait_full(pool, "mask1", k - 1)
                            for j in range(2):
                                nc.gpsimd.tensor_copy(
                                    hot_x[:, into(k), j].rearrange("p a (e r) -> p (a e) r", r=R),
                                    hot[:, j].rearrange("p a (e o) -> p (a e) o", o=1).to_broadcast([P, NA * NE, R]))\
                                    .then_inc(hot_wide, 1)
                        if k < preps and 21 <= o < 21 + NA:
                            a = o - 21
                            wait_read(pool, f"f{a}", k)
                            edge = nf[:, WOFF[a] + PAD + P * a:WOFF[a] + PAD + P * a + P]
                            nc.gpsimd.tensor_tensor(edge, edge, causal[:, :], ALU.add).then_inc(nf_done, 1)
                        if k < preps and o in (34, 43):
                            for a in ((0, 1), (2, 3))[o == 43]:
                                pool.wait_ge(selected, NA * k + a + 1)
                                edge = wk_sel[:, WOFF[a] + PAD + P * a:WOFF[a] + PAD + P * a + P]
                                link(nc.gpsimd.affine_select(out=edge, in_=edge, compare_op=ALU.not_equal, fill=0.0,
                                                             base=0, pattern=[[-1, P]], channel_multiplier=1))
                                if not setup:
                                    pool.wait_ge(masked, NH * NA * k)
                                nc.gpsimd.tensor_tensor(mask[:, into(k), OFF[a]:OFF[a + 1]],
                                                        nf[:, WOFF[a] + PAD:WOFF[a + 1]],
                                                        wk_sel[:, WOFF[a] + PAD:WOFF[a + 1]], ALU.add)\
                                    .then_inc(mask_done, 1)
                        if k < steps:
                            for f in range(NF):
                                if o == dict((n, q) for n, q, _ in FFN_JOBS)[f"h{f}1"] + 1:
                                    wait_read(pool, f"h{f}1", k)
                                    if f == 0 and k >= 1:
                                        wait_full(pool, "down", k - 1)
                                    nc.gpsimd.tensor_tensor(hsum[:, f, :], h[:, 2 * (f % 2), :], h[:, 2 * (f % 2) + 1, :],
                                                            ALU.add).then_inc(h_sum, 1)

                @block.scalar
                def _(act):
                    chain = [0]

                    def link(ins):
                        chain[0] += 1
                        ins.then_inc(act_chain, 1)

                    def copy(dst, src, name, k, last=True, **kw):
                        ins = nc.scalar.activation(dst, src, ACT.Identity, **kw)
                        ins.then_inc(act_read if last else act_chain, 1)

                    if setup:
                        wait_full(act, "w_attn", 0)
                        m = m_bank("w_attn", 0)
                        copy(wq[:, :].rearrange("c (d h) -> c d h", d=HD), m[:, 0:128].rearrange("c (h d) -> c d h", d=HD),
                             "w_attn", 0, False)
                        copy(wk[:, :].rearrange("c (d h) -> c d h", d=HD),
                             m[:, 128:256].rearrange("c (h d) -> c d h", d=HD), "w_attn", 0, False)
                        copy(wv[:, :], m[:, 256:384], "w_attn", 0)
                        wait_full(act, "w_in", 0)
                        copy(wi_t[:, :], m_bank("w_in", 0)[:, :], "w_in", 0)
                        wait_full(act, "w_out", 0)
                        copy(wo_t[:, :, :].rearrange("p f c -> p (f c)"), m_bank("w_out", 0)[:, :], "w_out", 0)
                        wait_full(act, "lora_b", 0)
                        copy(b_t[:, :], m_bank("lora_b", 0)[:, :], "lora_b", 0)
                        wait_full(act, "small", 0)
                        m = m_bank("small", 0)
                        copy(a_t[:, :], m[:, 0:128], "small", 0, False)
                        copy(wp_t[:, :], m[:, 128:256], "small", 0, False)
                        copy(gate_t[:, :], m[:, 256:264], "small", 0, False)
                        copy(bi_col[:, :], m[:, 264:268], "small", 0, False)
                        copy(bqk_col[:, 0:1], m[:, 268:269], "small", 0, False, scale=SCALE)
                        copy(bqk_col[:, 1:2], m[:, 269:270], "small", 0)
                        wait_full(act, "rows", 0)
                        copy(bias_b[:, :], m_bank("rows", 0)[:, 0:P + NE], "rows", 0)

                    for t in range(end):
                        k, o = divmod(t, NU)
                        u = t - 2
                        if 0 <= u < NU * steps:
                            a, h0, g = UNITS[u % NU]
                            act.wait_ge(turned, u + 1)
                            if u >= NP_RING:
                                act.wait_ge(summed, u - NP_RING + 1)
                            w = P * (a + 1) * g
                            nc.scalar.activation(pr[:, u % NP_RING, 0:w], ps_t[u % 2][:, 0:w], ACT.Exp, scale=-1.0)\
                                .then_inc(weighed, 1)
                        if k < preps and o == 10:
                            act.wait_ge(less_done, k + 1)
                            nc.scalar.activation(expd[:, :, :], less[:, :, :], ACT.Exp).then_inc(exp_done, 1)
                        for name, n in plan.at.get(t, []):
                            if plan.reads[name, n][0] != "act":
                                continue
                            wait_full(act, name, n)
                            m = m_bank(name, n)
                            if name == "xt":
                                if n >= 1 and not setup:
                                    wait_full(act, f"h{NF - 1}1", n - 1)
                                copy(xnt[:, into(n), :], m[:, :], name, n)
                            elif name in ("q", "k"):
                                j = ("q", "k").index(name)
                                if n >= 1:
                                    act.wait_ge(split, 2 * n)
                                if setup:
                                    wait_read(act, "small", 0)
                                copy(qk32[:, j, :], m[:, :], name, n, bias=bqk_col[:, j:j + 1],
                                     scale=(SCALE, 1.0)[j])
                            elif name[0] == "f":
                                a = int(name[1])
                                if n >= 1 and a == 0:
                                    act.wait_ge(mask_done, NA * n)
                                if setup:
                                    act.wait_ge(const, 2)
                                copy(nf[:, WOFF[a] + PAD:WOFF[a + 1]], m[:, 0:P * (a + 1)], name, n, scale=-1.0)
                            elif name == "z":
                                if n >= 1:
                                    wait_read(act, "mask1", n - 1)
                                copy(z[:, :], m[:, :], name, n)
                            elif name[0] == "h":
                                f, j = int(name[1]), int(name[2])
                                if NF * n + f >= 2:
                                    act.wait_ge(h_sum, NF * n + f - 1)
                                nc.scalar.activation(h[:, 2 * (f % 2) + j, :], m[:, :], ACT.Relu, bias=bi_col[:, f:f + 1])\
                                    .then_inc(act_read, 1)
                            elif name[0:2] == "yt":
                                a = int(name[2])
                                if n >= 1 and a in (0, 3):
                                    wait_full(act, ("proj0", "proj1")[a == 3], n - 1)
                                copy(yt[:, a, :], m[:, 0:P], name, n)

                @block.tensor
                def _(pe):
                    def fill(name, n):
                        i_job = plan.number[name, n]
                        if i_job >= 3:
                            wait_read(pe, *plan.order[i_job - 3])
                        m = m_bank(name, n)
                        c = into(n)
                        if name == "w_attn":
                            pe.wait_ge(w_in, 16 * 16)
                            pe.wait_ge(const, 1)
                            for j in range(3):
                                last = nc.tensor.transpose(m[:, P * j:P * j + P], raw_attn[:, j, :], ident[:, :])
                        elif name == "w_in":
                            for f in range(NF):
                                last = nc.tensor.transpose(m[:, P * f:P * f + P], raw_wi[:, f, :], ident[:, :])
                        elif name == "w_out":
                            for f in range(NF):
                                last = nc.tensor.transpose(m[:, P * f:P * f + P], raw_wo[:, P * f:P * f + P], ident[:, :])
                        elif name == "lora_b":
                            for f in range(NF):
                                last = nc.tensor.transpose(m[:, P * f:P * f + P],
                                                           raw_b[:, f].rearrange("p e r -> p (e r)"), ident[:, :])
                        elif name == "small":
                            nc.tensor.transpose(m[:, 0:P], raw_a, ident[:, :])
                            nc.tensor.transpose(m[:, P:2 * P], raw_wp, ident[:, :])
                            nc.tensor.transpose(m[:, 256:264], raw_gate[:, :], ident[0:NE, 0:NE])
                            nc.tensor.transpose(m[:, 264:268], raw_bi[:, :], ident[0:NF, 0:NF])
                            pe.wait_ge(w_prep, 3)
                            last = nc.tensor.transpose(m[:, 268:270], bqk_dh[:, :], ident[0:2, 0:2])
                        elif name == "rows":
                            last = nc.tensor.matmul(m[:, 0:P + NE], ones[0:1, 0:P], bias_row[:, :], start=True, stop=True)
                        elif name == "xt":
                            pe.wait_ge(xn_done, NA * (n + 1))
                            for a in range(NA):
                                last = nc.tensor.transpose(m[:, P * a:P * a + P], xn[:, a, :], ident[:, :])
                        elif name in ("q", "k"):
                            wait_read(pe, "xt", n)
                            last = nc.tensor.matmul(m[:, :], (wq if name == "q" else wk)[:, :], xnt[:, c, :],
                                                    start=True, stop=True)
                        elif name == "v":
                            for a in range(NA):
                                last = nc.tensor.matmul(m[:, P * a:P * a + P], xnt[:, c, P * a:P * a + P], wv[:, :],
                                                        start=True, stop=True)
                        elif name == "gate":
                            if setup:
                                wait_read(pe, "small", 0)
                            for a in range(NA):
                                last = nc.tensor.matmul(m[:, NE * a:NE * a + NE], xnt[:, c, P * a:P * a + P], gate_t[:, :],
                                                        start=True, stop=True)
                        elif name[0] == "s":
                            j = int(name[1])
                            pe.wait_ge(stacked, 192 * (n + 1))
                            last = nc.tensor.matmul(m[:, 0:T - P * j], ks[:, c, 0, P * j:P * j + P], qs[:, c, 0, P * j:T],
                                                    start=True, stop=True)
                        elif name[0] == "f":
                            a = int(name[1])
                            pe.wait_ge(scanned, NA * (n + 1))
                            for j in range(a + 1):
                                at = FOFF[j] + P * (a - j)
                                last = nc.tensor.transpose(m[:, P * j:P * j + P], ft[:, at:at + P], ident[:, :])
                        elif name == "z":
                            last = nc.tensor.matmul(m[:, :], a_t[:, :], xnt[:, n, :], start=True, stop=True)
                        elif name[0:4] == "mask":
                            j = int(name[4])
                            for a in range(NA):
                                last = nc.tensor.matmul(m[:, P * a:P * a + P], hot_x[:, n, j, a, :], ident16[:, :],
                                                        start=True, stop=True)
                        elif name[0] == "h":
                            f, j = int(name[1]), int(name[2])
                            wait_read(pe, f"mask{j}", n)
                            nc.tensor.matmul(m[:, :], wi_t[:, P * f:P * f + P], xnt[:, n, :], start=True, stop=False)
                            last = nc.tensor.matmul(m[:, :], b_t[:, P * f:P * f + P], zm[:, j, :], start=False, stop=True)
                        elif name == "down":
                            pe.wait_ge(h_sum, NF * (n + 1))
                            for a in range(NA):
                                for f in range(NF):
                                    nc.tensor.matmul(m[:, P * a:P * a + P], hsum[:, f, P * a:P * a + P], wo_t[:, f, :],
                                                     start=(f == 0), stop=False)
                                last = nc.tensor.matmul(m[:, P * a:P * a + P], ones[0:1, 0:P], bo2_row[:, :],
                                                        start=False, stop=True)
                        elif name[0:2] == "yt":
                            a = int(name[2])
                            pe.wait_ge(normed, NA * n + a + 1)
                            last = nc.tensor.transpose(m[:, 0:P], y[:, a, :, :].rearrange("p h d -> p (h d)"), ident[:, :])
                        elif name[0:4] == "proj":
                            lo, hi = ((0, NA - 1), (NA - 1, NA))[int(name[4])]
                            wait_read(pe, f"yt{hi - 1}", n)
                            for a in range(lo, hi):
                                at = P * (a - lo)
                                nc.tensor.matmul(m[:, at:at + P], yt[:, a, :], wp_t[:, :], start=True, stop=False)
                                last = nc.tensor.matmul(m[:, at:at + P], ones[0:1, 0:P], bp_row[:, :],
                                                        start=False, stop=True)
                        last.then_inc(m_full, 1)

                    def score(u):
                        k, o = divmod(u, NU)
                        a, h0, g = UNITS[o]
                        w = P * (a + 1)
                        if o == 0 and k >= 1:
                            pe.wait_ge(stacked, 192 * k)
                        if u >= 2:
                            kk, oo = divmod(u - 2, NU)
                            pe.wait_ge(masked, NH * NA * kk + HEADS_TO[oo])
                        for j in range(g):
                            last = nc.tensor.matmul(ps_s[u % 2][:, w * j:w * j + w], qs[:, k, h0 + j, P * a:P * a + P],
                                                    ks[:, k, h0 + j, 0:w], start=True, stop=True)
                        last.then_inc(scored, 1)

                    def turn(u):
                        k, o = divmod(u, NU)
                        a, h0, g = UNITS[o]
                        pe.wait_ge(shifted, NH * NA * k + HEADS_TO[o])
                        if u >= 2:
                            pe.wait_ge(weighed, u - 1)
                        for j in range(g * (a + 1)):
                            last = nc.tensor.transpose(ps_t[u % 2][:, P * j:P * j + P],
                                                       ar[:, u % NA_RING, P * j:P * j + P], ident[:, :])
                        last.then_inc(turned, 1)

                    def weigh(u):
                        k, o = divmod(u, NU)
                        a, h0, g = UNITS[o]
                        pe.wait_ge(weighed, u + 1)
                        if h0 == 0 and NA * k + a >= 1:
                            pe.wait_ge(normed, NA * k + a)
                        for j in range(g):
                            hh = h0 + j
                            for c in range(a + 1):
                                at = P * ((a + 1) * j + c)
                                last = nc.tensor.matmul(ps_o[:, VW * hh:VW * hh + VW], pr[:, u % NP_RING, at:at + P],
                                                        va[:, k, c, VW * hh:VW * hh + VW], start=(c == 0), stop=(c == a))
                        last.then_inc(summed, 1)

                    if setup:
                        for name in SETUP_JOBS:
                            fill(name, 0)
                    for t in range(end):
                        for name, n in plan.at.get(t, []):
                            fill(name, n)
                        if t < NU * steps:
                            score(t)
                        if 0 <= t - 2 < NU * steps:
                            turn(t - 2)
                        if 0 <= t - 4 < NU * steps:
                            weigh(t - 4)

                @block.vector
                def _(dve):
                    chain = [0]

                    def link(ins):
                        chain[0] += 1
                        ins.then_inc(dve_chain, 1)
                        dve.wait_ge(dve_chain, chain[0])

                    if setup:
                        nc.vector.memset(ones[:, :], 1.0).then_inc(w_prep, 1)
                        for e in range(NE):
                            link(nc.vector.memset(rank[:, :, e:e + 1], float(NE - e)))
                        dve.wait_ge(w_in, 16 * 16)
                        nc.vector.tensor_copy(bqk_dh[:, :].rearrange("t (d h) -> t d h", d=HD),
                                              raw_bqk[:, :].rearrange("t (h d) -> t d h", d=HD)).then_inc(w_prep, 1)
                        nc.vector.tensor_scalar(bo2_row[:, :], bo_row[:, :], 2.0, None, ALU.mult).then_inc(w_prep, 1)

                    def moments(n):
                        c = into(n)
                        dve.wait_ge(x_in, 16 * (n + 1))
                        for a in range(NA):
                            last = nc.vector.bn_stats(stats[:, a, :], xs[:, c, a, :])
                            last.then_inc(dve_chain, 1)
                            chain[0] += 1
                        dve.wait_ge(dve_chain, chain[0])
                        for a in range(NA):
                            nc.vector.bn_aggr(mv[:, a, :], stats[:, a, :]).then_inc(dve_chain, 1)
                            chain[0] += 1
                        dve.wait_ge(dve_chain, chain[0])
                        nc.vector.tensor_scalar(var[:, :], mv[:, :, 1], EPS, None, ALU.add).then_inc(varred, 1)

                    def normalise(n):
                        dve.wait_ge(rooted, n + 1)
                        if n >= 1:
                            wait_full(dve, "xt", n - 1)
                        for a in range(NA):
                            nc.vector.tensor_scalar(xn[:, a, :], xs[:, into(n), a, :], mv[:, a, 0:1], rstd[:, a:a + 1],
                                                    ALU.subtract, ALU.mult).then_inc(xn_done, 1)

                    def wide(col):
                        return col.rearrange("p (a o) -> p a o", o=1).to_broadcast([P, NA, NE])

                    def choose(j):
                        link(nc.vector.tensor_reduce(best[:, j, :], logit[:, :, :], AX, ALU.max))
                        link(nc.vector.tensor_tensor(eq[:, :, :], logit[:, :, :], wide(best[:, j, :]), ALU.is_equal))
                        link(nc.vector.tensor_tensor(tie[:, :, :], eq[:, :, :], rank[:, :, :], ALU.mult))
                        link(nc.vector.tensor_reduce(best[:, 2 + j, :], tie[:, :, :], AX, ALU.max))
                        ins = nc.vector.tensor_tensor(hot[:, j], tie[:, :, :], wide(best[:, 2 + j, :]), ALU.is_equal)
                        return ins

                    def route(n):
                        wait_full(dve, "gate", n)
                        if setup:
                            wait_read(dve, "rows", 0)
                        if n >= 1:
                            dve.wait_ge(hot_wide, 2 * n)
                        m = m_bank("gate", n)
                        nc.vector.tensor_tensor(
                            logit[:, :, :], m[:, 0:NA * NE].rearrange("p (a e) -> p a e", e=NE),
                            bias_b[:, P:P + NE].rearrange("p (o e) -> p o e", o=1).to_broadcast([P, NA, NE]), ALU.add)\
                            .then_inc(dve_read, 1)
                        dve.wait_ge(dve_read, plan.reads["gate", n][1])
                        link(choose(0))
                        link(nc.vector.tensor_tensor(less[:, :, 0:NE], logit[:, :, :], wide(best[:, 0, :]), ALU.subtract))
                        link(nc.vector.tensor_scalar(eq[:, :, :], hot[:, 0], -BIG, None, ALU.mult))
                        link(nc.vector.tensor_tensor(logit[:, :, :], logit[:, :, :], eq[:, :, :], ALU.add))
                        choose(1).then_inc(hot_done, 1)
                        nc.vector.tensor_tensor(less[:, :, NE:NE + 1].rearrange("p a o -> p (a o)"), best[:, 1, :],
                                                best[:, 0, :], ALU.subtract).then_inc(less_done, 1)

                    def share(n):
                        dve.wait_ge(exp_done, n + 1)
                        link(nc.vector.tensor_reduce(den[:, :], expd[:, :, 0:NE], AX, ALU.add))
                        link(nc.vector.reciprocal(den[:, :], den[:, :]))
                        c = into(n)
                        link(nc.vector.tensor_scalar(vsum[:, c, :], expd[:, :, NE:NE + 1].rearrange("p a o -> p (a o)"),
                                                     1.0, None, ALU.add))
                        link(nc.vector.tensor_tensor(vsum[:, c, :], vsum[:, c, :], den[:, :], ALU.mult))

                    def forget(n, j):
                        wait_full(dve, f"s{j}", n)
                        if j == 0:
                            if setup:
                                dve.wait_ge(const, 2)
                            if n >= 1:
                                wait_full(dve, f"f{NA - 1}", n - 1)
                        w = T - P * j
                        nc.vector.scalar_tensor_tensor(out=s0[:, FOFF[j]:FOFF[j] + w], in0=m_bank(f"s{j}", n)[:, 0:w],
                                                       scalar=0.0, in1=later[:, min(j, 1), 0:w], op0=ALU.max,
                                                       op1=ALU.mult).then_inc(dve_read, 1)
                        link(nc.vector.memset(ft[:, FOFF[j]:FOFF[j] + 1], 0.0))
                        dve.wait_ge(dve_read, plan.reads[f"s{j}", n][1])
                        nc.vector.tensor_tensor_scan(ft[:, FOFF[j] + 1:FOFF[j] + w], ones[:, 0:w - 1],
                                                     s0[:, FOFF[j]:FOFF[j] + w - 1], 0.0, ALU.mult, ALU.add)\
                            .then_inc(scanned, 1)

                    SEL = []
                    for pair in ((0, 1), (2, 3)):
                        for r in range(ROUNDS):
                            SEL += [("max", a, r) for a in pair] + [("mark", a, r) for a in pair]
                        SEL += [("pen", a, 0) for a in pair]
                    done = {}
                    for x_ in SEL:
                        done[x_] = len(done) + 1

                    def prune(n, j):
                        kind, a, r = SEL[j]
                        base = len(SEL) * n
                        lo, hi = WOFF[a], WOFF[a + 1]
                        src = nf if r == 0 else wk_sel
                        if kind == "max":
                            if r == 0:
                                dve.wait_ge(nf_done, NA * n + a + 1)
                                if n >= 1:
                                    dve.wait_ge(mask_done, NA * n)
                            else:
                                dve.wait_ge(sel, base + done["mark", a, r - 1])
                            nc.vector.max(top8[:, a, :], src[:, lo:hi]).then_inc(sel, 1)
                        elif kind == "mark":
                            dve.wait_ge(sel, base + done["max", a, r])
                            nc.vector.match_replace(wk_sel[:, lo:hi], top8[:, a, :], src[:, lo:hi], MARK).then_inc(sel, 1)
                        else:
                            dve.wait_ge(sel, base + done["mark", a, ROUNDS - 1])
                            nc.vector.tensor_scalar(wk_sel[:, lo:hi], wk_sel[:, lo:hi], MARK / 2, -BIG, ALU.is_gt, ALU.mult)\
                                .then_inc(selected, 1)
                            nc.vector.memset(top8[:, a, 0:1], 0.0).then_inc(sel, 1)

                    START, SLOTS = 24, 19

                    for t in range(end):
                        k, o = divmod(t, NU)
                        if k < steps:
                            a, h0, g = UNITS[o]
                            w = P * (a + 1)
                            dve.wait_ge(scored, t + 1)
                            if t >= NA_RING:
                                dve.wait_ge(turned, t - NA_RING + 1)
                            if h0 == 0 and k >= 1:
                                dve.wait_ge(mask_done, NA * (k - 1) + a + 1)
                            for j in range(g):
                                nc.vector.tensor_tensor_reduce(
                                    out=ar[:, t % NA_RING, w * j:w * j + w], in0=ps_s[t % 2][:, w * j:w * j + w],
                                    in1=mask[:, k, OFF[a]:OFF[a + 1]], scale=1.0, scalar=MARK, op0=ALU.add, op1=ALU.max,
                                    accum_out=mx[:, t % NA_RING, j:j + 1]).then_inc(masked, 1)
                        for kk in range(steps):
                            for a in range(NA):
                                if t == NU * kk + LAST[a] + 4:
                                    dve.wait_ge(summed, NU * kk + LAST[a] + 1)
                                    if kk >= 1:
                                        wait_full(dve, f"yt{a}", kk - 1)
                                    o3 = ps_o[:, 0:NH * VW].rearrange("p (h d) -> p h d", d=VW)
                                    link(nc.vector.reciprocal(rec[:, :].rearrange("p (h o) -> p h o", o=1),
                                                              o3[:, :, HD:VW]))
                                    nc.vector.tensor_tensor(
                                        y[:, a, :, :], o3[:, :, 0:HD],
                                        rec[:, :].rearrange("p (h o) -> p h o", o=1).to_broadcast([P, NH, HD]), ALU.mult)\
                                        .then_inc(normed, 1)
                        if k < preps:
                            if o == 0:
                                moments(k)
                            if o == 2:
                                normalise(k)
                            if o == 11:
                                share(k)
                            if START <= o < START + SLOTS:
                                for j in range(len(SEL) * (o - START) // SLOTS, len(SEL) * (o - START + 1) // SLOTS):
                                    prune(k, j)
                        for name, n in plan.at.get(t, []):
                            if plan.reads[name, n][0] != "dve":
                                continue
                            m = m_bank(name, n)
                            if name == "v":
                                wait_full(dve, name, n)
                                if setup:
                                    wait_read(dve, "rows", 0)
                                    dve.wait_ge(const, 2)
                                elif n >= 1:
                                    dve.wait_ge(summed, NU * n)
                                for a in range(NA):
                                    ins = nc.vector.tensor_tensor(
                                        va[:, into(n), a, :].rearrange("p (h d) -> p h d", d=VW)[:, :, 0:HD],
                                        m[:, P * a:P * a + P].rearrange("p (h d) -> p h d", d=HD),
                                        bias_b[:, 0:P].rearrange("p (h d) -> p h d", d=HD), ALU.add)
                                ins.then_inc(dve_read, 1)
                            elif name == "gate":
                                route(n)
                            elif name[0] == "s":
                                forget(n, int(name[1]))
                            elif name[0:4] == "mask":
                                j = int(name[4])
                                wait_full(dve, name, n)
                                wait_read(dve, "z", n)
                                if n >= 1:
                                    wait_full(dve, f"h{NF - 1}1", n - 1)
                                nc.vector.tensor_tensor(zm[:, j, :], m[:, :], z[:, :], ALU.mult).then_inc(dve_read, 1)
                            elif name == "down":
                                wait_full(dve, name, n)
                                for a in range(NA):
                                    ins = nc.vector.scalar_tensor_tensor(
                                        out=down[:, a, :], in0=m[:, P * a:P * a + P], scalar=vsum[:, n, a:a + 1],
                                        in1=xs[:, n, a, :], op0=ALU.mult, op1=ALU.add)
                                ins.then_inc(dve_read, 1)
                            elif name[0:4] == "proj":
                                lo, hi = ((0, NA - 1), (NA - 1, NA))[int(name[4])]
                                wait_full(dve, name, n)
                                wait_read(dve, "down", n)
                                if n >= 1:
                                    dve.wait_ge(stored, 32 * n)
                                nc.vector.tensor_tensor(res[:, lo:hi, :].rearrange("p a c -> p (a c)"),
                                                        m[:, 0:P * (hi - lo)],
                                                        down[:, lo:hi, :].rearrange("p a c -> p (a c)"), ALU.add)\
                                    .then_inc(dve_read, 1)

            with nc.Block() as clear:
                @clear.sync
                def _(sp):
                    for one in s.values():
                        sp.sem_clear(one)

        run_block(0, 0, 1, setup=True)
        with nc.Fori(0, B // 2 - 1) as i:
            run_block(i, 2, 2)
        run_block(B // 2 - 1, 2, 1)


_INS = ['L0_attn_x', 'L0_attn_w_attn', 'L0_attn_b_attn', 'L0_attn_w_proj', 'L0_attn_b_proj', 'L0_ffn_wi', 'L0_ffn_bi',
        'L0_ffn_wo', 'L0_ffn_bo', 'L0_ffn_lora_A', 'L0_ffn_lora_B', 'L0_ffn_gate_w', 'L0_ffn_gate_b']


def kernel(**inputs):
    import numpy as _np
    import concourse.bacc as _bacc
    from concourse import mybir as _mybir
    from concourse.bass_utils import run_bass_kernel_spmd as _run
    nc = _bacc.Bacc("TRN2", target_bir_lowering=False, num_devices=1)
    arrays, args = {}, []
    for name in _INS:
        a = _np.ascontiguousarray(inputs[name])
        arrays[f"in_{name}"] = a
        args.append(nc.dram_tensor(f"in_{name}", a.shape, _mybir.dt.from_np(a.dtype), kind="ExternalInput").ap())
    out = nc.dram_tensor("out", (8, 512, 128), _mybir.dt.float32, kind="ExternalOutput").ap()
    build(nc, *args, out)
    r = _run(nc, [arrays], core_ids=[0])
    return r.results[0]["out"]
```

```python
from contextlib import ExitStack

import concourse.bass as bass
from concourse import mybir

F32 = mybir.dt.float32
BF16 = mybir.dt.bfloat16
ALU = mybir.AluOpType
ACT = mybir.ActivationFunctionType
AX = mybir.AxisListType.X

P = 128
B, T, C = 8, 512, 128
XN = 4
STEPS = 4
NH, HD = 16, 8
NA = T // P
HALF = ((0, 1), (2, 3))
FF, NE, R = 512, 8, 16
NF = FF // P
KEEP = max(1, int(T * 0.2)) - 1
SCALE = 1.0 / HD ** 0.5
EPS = 1e-5
BIG = 1.0e30
MARK = -3.0e38
FAST = 2
SLACK = 8 * FAST
HALVINGS = 8
REACH = 1.25
AIM = KEEP - SLACK / 2 + 0.5
PADS = SLACK
ROUNDS = -(-KEEP // 8)
WIDE = PADS + T
VW = HD + 1
OW = 512 // NH
MOVED = 56

Q_PART = (0, 0, 1, 1, 0, 2)
K_PART = (0, 1, 0, 1, 2, 0)
STACK = 8 * len(Q_PART)
ROWS = 96

UNITS = [(a, h, 4 // w) for a, w in ((0, 1), (1, 2), (2, 4), (3, 4)) for h in range(0, NH, 4 // w)]
NU = len(UNITS)
LAST = [max(u for u in range(NU) if UNITS[u][0] == a) for a in range(NA)]
HEADS_TO = [sum(x[2] for x in UNITS[:u + 1]) for u in range(NU)]
OFF = [P * a * (a + 1) // 2 for a in range(NA + 1)]
FOFF = [sum(T - P * x for x in range(c)) for c in range(NA + 1)]


NS_RING, NT_RING, NM_RING = 3, 2, 2
NA_RING, NP_RING = 6, 4
LAG_T, LAG_P = 3, 6
YT_LAG = 3
TAIL = 12

HIDDEN_AT = (14, 17, 20, 23)
FFN_JOBS = [("z", 1, "act"), ("mask0", 3, "dve"), ("mask1", 4, "dve")] + \
    [(f"h{f}{j}", HIDDEN_AT[f] + j, "act") for f in range(NF) for j in range(2)] + \
    [("down0", 28, "dve"), ("down1", 30, "dve")]
ATT_JOBS = [(f"yt{a}", LAST[a] + LAG_P + YT_LAG, "act") for a in range(NA)] + \
    [("proj0", 40, "dve"), ("proj1", LAST[3] + LAG_P + YT_LAG + 2, "dve")]
PREP_AT = {
    "moments": (0, -18), "root": (0, -17), "norm": (1, -15), "xt": (2, -12), "q": (3, -10), "k": (4, -8),
    "rest_q": (4, -9), "second_q": (5, -8), "third_q": (6, -7),
    "rest_k": (5, -7), "second_k": (6, -6), "third_k": (7, -5),
    "gate": (8, -3), "route": (8, -2), "choices": (9, 0), "share": (10, 2),
    "s0": (11, 5), "s1": (12, 6), "s2": (13, 7), "s3": (14, 8), "v": (15, 9),
    "scan0": (12, 6), "scan1": (13, 7), "scan2": (14, 8), "scan3": (15, 9),
    "f0": (16, 10), "f1": (17, 11), "f2": (18, 12), "f3": (19, 13),
    "search": (20, 14),
    "under_narrow": (36, 30), "under_wide": (36, 31), "reach": (37, 31),
    "marks_narrow": (38, 32), "marks_wide": (38, 33),
    "top0_narrow": (39, 33), "top0_wide": (39, 34), "replace0_narrow": (39, 35), "replace0_wide": (39, 36),
    "top1_narrow": (40, 36), "top1_wide": (40, 37), "replace1_narrow": (40, 38), "replace1_wide": (40, 39),
    "flag": (41, 40),
    "mask_0": (42, 41), "mask_1": (42, 42), "mask_2": (43, 43), "mask_3": (44, 44),
}
PREP_JOBS = [("xt", "act"), ("q", "act"), ("k", "act"), ("gate", "dve"), ("v", "dve")] + \
    [(f"s{c}", "act") for c in range(NA)] + [(f"f{a}", "dve") for a in range(NA)] + [("flag", "dve")]


EARLY = ("moments", "root", "norm", "xt", "q", "k", "rest_q", "second_q", "third_q", "rest_k", "second_k", "third_k",
         "gate", "route", "choices", "share")


SETUP_JOBS = ["w_attn", "w_in", "w_out", "lora_b", "small", "rows"]


class Plan:

    def __init__(self, steps, preps, setup):
        self.setup = setup
        self.late = range(preps)
        self.early = range(0 if setup else 1, preps + 1)
        jobs = [(-1, (name, 0), "act") for name in SETUP_JOBS] if setup else []
        for k in range(steps):
            jobs += [(NU * k + o, (name, k), who) for name, o, who in FFN_JOBS + ATT_JOBS]
        jobs += [(self.slot(name, n), (name, n), who) for name, who in PREP_JOBS
                 for n in (self.early if name in EARLY else self.late)]
        jobs.sort(key=lambda x: x[0])
        self.at, self.number, self.place, self.reads, self.last = {}, {}, {}, {}, []
        counts = {"act": 0, "dve": 0}
        for i, (t, key, who) in enumerate(jobs):
            self.at.setdefault(t, []).append(key)
            self.number[key] = i
            if key[0][0] == "h" and key[0][2] == "1":
                self.place[key] = self.place[key[0][:2] + "0", key[1]]
                self.last[self.place[key]] = key
            else:
                self.place[key] = len(self.last)
                self.last.append(key)
            counts[who] += 1
            self.reads[key] = (who, counts[who])

    def slot(self, name, n):
        if n not in (self.early if name in EARLY else self.late):
            return None
        return PREP_AT[name][0 if self.setup and n == 0 else 1] + NU * n


def build(nc, x, w_attn, b_attn, w_proj, b_proj, wi, bi, wo, bo, lora_a, lora_b, gate_w, gate_b, out):
    ctx = ExitStack()
    with ctx:
        def sb(name, shape, dt=F32):
            return ctx.enter_context(nc.sbuf_tensor(name, shape, dt))

        def sem(name):
            return ctx.enter_context(nc.semaphore(name))

        ident = sb("ident", [P, P])
        ident16 = sb("ident16", [P, P], BF16)
        ones = sb("ones", [P, T])
        causal = sb("causal", [P, P])
        minus_half = sb("minus_half", [P, NA])
        half_mark = sb("half_mark", [P, 1])
        not_first = sb("not_first", [P, 2])
        rank = sb("rank", [P, NA, NE])
        ar = sb("ar", [P, NA_RING, T])
        raw = ar[:, :, :].rearrange("p n t -> p (n t)")
        raw_attn = raw[:, 0:384].rearrange("p (t c) -> p t c", t=3)
        raw_wi = raw[:, 384:896].rearrange("p (f c) -> p f c", f=NF)
        raw_wo = raw[:, 896:1408]
        raw_b = raw[:, 1408:1920].rearrange("p (f e r) -> p f e r", f=NF, e=NE)
        raw_a = raw[:, 1920:2048]
        raw_wp = raw[:, 2048:2176]
        raw_gate = sb("raw_gate", [NE, C])
        raw_bi = sb("raw_bi", [NF, P])
        raw_bqk = sb("raw_bqk", [2, P])
        bqk_dh = sb("bqk_dh", [2, P])
        bias_row = sb("bias_row", [1, P + NE])
        bp_row = sb("bp_row", [1, C])
        bo_row = sb("bo_row", [1, C])
        bo2_row = sb("bo2_row", [1, C])
        wq = sb("wq", [C, P])
        wk = sb("wk", [C, P])
        wv = sb("wv", [C, P])
        wi_t = sb("wi_t", [C, FF])
        wo_t = sb("wo_t", [P, NF, C])
        b_t = sb("b_t", [NE * R, FF])
        a_t = sb("a_t", [C, NE * R])
        wp_t = sb("wp_t", [P, C])
        gate_t = sb("gate_t", [C, NE])
        bi_col = sb("bi_col", [P, NF])
        bqk_col = sb("bqk_col", [P, 2])
        bias_b = sb("bias_b", [P, P + NE])
        xs = sb("xs", [P, XN, NA, C])
        stats = sb("stats", [P, NA, 6])
        mv = sb("mv", [P, NA, 2])
        minus_mean = sb("minus_mean", [P, NA])
        shift = sb("shift", [P, NA])
        var = sb("var", [P, NA])
        rstd = sb("rstd", [P, NA])
        xn = sb("xn", [P, NA, C])
        xnt = sb("xnt", [C, 2, T])
        qk32 = sb("qk32", [P, 2, T])
        parts = sb("parts", [P, 2, 3, T], BF16)
        qs = sb("qs", [ROWS, 2, NH, T], BF16)
        ks = sb("ks", [ROWS, 2, NH, T], BF16)
        va = sb("va", [P, 2, NA, (NH - 1) * VW + MOVED])
        s0 = sb("s0", [P, FOFF[NA]])
        ft = sb("ft", [P, FOFF[NA]])
        nf = sb("nf", [P, OFF[NA]])
        work = sb("work", [P, NA, WIDE])
        junk = sb("junk", [P, 2, T], BF16)
        greatest = sb("greatest", [P, NA])
        halves = sb("halves", [P, HALVINGS, NA])
        cut = sb("cut", [P, NA])
        above = sb("above", [P, NA])
        step_to = sb("step_to", [P, NA])
        count = sb("count", [P, NA])
        bad = sb("bad", [P, 2, NA])
        flag = sb("flag", [1, 1])
        flag_i = sb("flag_i", [1, 1], mybir.dt.int32)
        pads01 = sb("pads01", [P, NA, PADS])
        query = sb("query", [P, NA])
        reach = sb("reach", [P, NA])
        all_low = sb("all_low", [P, NA])
        few = sb("few", [P, NA])
        pad_no = sb("pad_no", [P, NA, PADS])
        top8 = sb("top8", [P, NA, 8])
        mask = sb("mask", [P, 2, OFF[NA]])
        logit = sb("logit", [P, NA, NE])
        less = sb("less", [P, NA, NE + 1])
        expd = sb("expd", [P, NA, NE + 1])
        eq = sb("eq", [P, NA, NE])
        tie = sb("tie", [P, NA, NE])
        hot = sb("hot", [P, 2, NA, NE])
        best = sb("best", [P, 4, NA])
        den = sb("den", [P, NA])
        vsum = sb("vsum", [P, 2, NA])
        rest = sb("rest", [P, 2, T])
        hot_x = sb("hot_x", [P, 2, 2, NA, NE * R], BF16)
        z = sb("z", [P, T])
        zm = sb("zm", [P, 2, T])
        h = sb("h", [P, 4, T])
        hsum = sb("hsum", [P, NF, T])
        down = sb("down", [P, NA, C])
        mx = sb("mx", [P, NA_RING, 4])
        pr = sb("pr", [P, NP_RING, T])
        rec = sb("rec", [P, NH])
        y = sb("y", [P, NA, NH, HD])
        yt = sb("yt", [P, NA, P])
        res = sb("res", [P, NA, C])

        def bank(name):
            return ctx.enter_context(nc.psum_tensor(name, [P, 512], F32))

        ps_s = [bank(f"ps_s{i}") for i in range(NS_RING)]
        ps_t = [bank(f"ps_t{i}") for i in range(NT_RING)]
        ps_o = bank("ps_o")
        ps_m = [bank(f"ps_m{i}") for i in range(NM_RING)]

        names = ["w_in", "x_in", "const", "w_prep", "scored", "masked", "shifted", "turned", "weighed",
                 "summed", "normed", "m_full", "act_read", "dve_read", "varred", "rooted", "xn_done",
                 "limited", "ruled", "centred", "split", "stacked", "less_done", "exp_done", "hot_done", "hot_wide", "scanned", "nf_done", "halved", "counted", "rested", "parted", "again",
                 "selected", "mask_done", "h_sum", "stored", "dve_chain", "pool_chain",
                 "act_chain", "sel", "zeroed"]
        s = {n: sem(n) for n in names}
        w_in, x_in, const, w_prep = s["w_in"], s["x_in"], s["const"], s["w_prep"]
        scored, masked, shifted, turned = s["scored"], s["masked"], s["shifted"], s["turned"]
        weighed, summed, normed = s["weighed"], s["summed"], s["normed"]
        m_full, act_read, dve_read = s["m_full"], s["act_read"], s["dve_read"]
        varred, rooted, xn_done, split, stacked = s["varred"], s["rooted"], s["xn_done"], s["split"], s["stacked"]
        less_done, exp_done, hot_done, hot_wide = s["less_done"], s["exp_done"], s["hot_done"], s["hot_wide"]
        scanned, nf_done, selected, mask_done = s["scanned"], s["nf_done"], s["selected"], s["mask_done"]
        h_sum, stored = s["h_sum"], s["stored"]
        dve_chain, pool_chain, act_chain, sel = s["dve_chain"], s["pool_chain"], s["act_chain"], s["sel"]
        zeroed, halved, counted, rested, parted = s["zeroed"], s["halved"], s["counted"], s["rested"], s["parted"]
        again, limited, ruled, centred = s["again"], s["limited"], s["ruled"], s["centred"]

        x_d = x.rearrange("b (a p) c -> b p a c", p=P)
        out_d = out.rearrange("b (a p) c -> b p a c", p=P)

        def run_block(i, steps, preps, setup=False):
            plan = Plan(steps, preps, setup)
            into = (lambda n: n % 2) if setup else (lambda n: (n + 1) % 2)
            x_into = (lambda n: n % XN) if setup else (lambda n: (n + 1) % XN)
            at = plan.slot
            nth = (lambda n: n) if setup else (lambda n: n - 1)
            end = NU * max(steps, preps) + TAIL

            def full(name, k):
                return plan.number[name, k] + 1

            def wait_full(eng, name, k):
                eng.wait_ge(m_full, full(name, k))

            def wait_read(eng, name, k):
                who, n = plan.reads[name, k]
                eng.wait_ge(act_read if who == "act" else dve_read, n)

            def m_bank(name, k):
                return ps_m[plan.place[name, k] % NM_RING]

            with nc.Block() as block:

                def store(sp, k, part):
                    wait_read(sp, ("proj0", "proj1")[part], k)
                    lo, hi = ((0, NA - 1), (NA - 1, NA))[part]
                    b = i * STEPS + k
                    sp.dma_start(out_d[bass.ds(b, 1), :, lo:hi, :].rearrange("o p a c -> p (o a) c"),
                                 res[:, lo:hi, :]).then_inc(stored, 16)

                @block.sync
                def _(sp):
                    if setup:
                        sp.dma_start(xs[:, 0, :, :], x_d[0]).then_inc(x_in, 16)
                        sp.dma_start(raw_attn, w_attn.rearrange("(t p) c -> p t c", p=P)).then_inc(w_in, 16)
                        sp.dma_start(raw_wi, wi.rearrange("(f p) c -> p f c", p=P)).then_inc(w_in, 16)
                        sp.dma_start(raw_wo, wo).then_inc(w_in, 16)
                        for f in range(NF):
                            sp.dma_start(raw_b[:, f], lora_b[:, P * f:P * f + P, :].rearrange("e p r -> p e r"))\
                                .then_inc(w_in, 16)
                        sp.dma_start(raw_a, lora_a.rearrange("e r c -> (e r) c")).then_inc(w_in, 16)
                        sp.dma_start(raw_wp, w_proj).then_inc(w_in, 16)
                        sp.dma_start(raw_gate[:, :], gate_w).then_inc(w_in, 16)
                        sp.dma_start(raw_bi[:, :], bi.rearrange("(f p) -> f p", p=P)).then_inc(w_in, 16)
                        sp.dma_start(raw_bqk[:, :], b_attn[0:2 * P].rearrange("(t p) -> t p", p=P)).then_inc(w_in, 16)
                        sp.dma_start(bias_row[:, 0:P], b_attn[2 * P:3 * P].rearrange("(o p) -> o p", o=1))\
                            .then_inc(w_in, 16)
                        sp.dma_start(bias_row[:, P:P + NE], gate_b.rearrange("(o p) -> o p", o=1)).then_inc(w_in, 16)
                        sp.dma_start(bp_row[:, :], b_proj.rearrange("(o p) -> o p", o=1)).then_inc(w_in, 16)
                        sp.dma_start(bo_row[:, :], bo.rearrange("(o p) -> o p", o=1)).then_inc(w_in, 16)
                    def fetch(n):
                        if nth(n) >= 1:
                            sp.wait_ge(x_in, 16 * nth(n))
                        if n >= XN - 1:
                            wait_read(sp, "down1", n - (XN - 1))
                        if setup:
                            b = n
                        elif n + 1 < STEPS:
                            b = i * STEPS + (n + 1)
                        else:
                            b = (n + 1 - STEPS) + (B - STEPS) - i * (B - STEPS)
                        sp.dma_start(xs[:, x_into(n), :, :],
                                     x_d[bass.ds(b, 1)].rearrange("o p a c -> p (o a) c")).then_inc(x_in, 16)

                    fetch(1)
                    for k in range(max(steps, preps)):
                        if k < preps:
                            for t in range(2):
                                if t == 0 and k >= 1:
                                    sp.wait_ge(scored, NU * k)
                                if setup:
                                    sp.wait_ge(zeroed, 2)
                                if nth(k) >= 0:
                                    sp.wait_ge(split, 2 * nth(k) + t + 1)
                                stack, part = ((qs, Q_PART), (ks, K_PART))[t]
                                for j in range(len(part)):
                                    sp.dma_start(stack[8 * j:8 * j + 8, into(k), :, :], parts[:, t, part[j], :])\
                                        .then_inc(stacked, 16)
                        if k >= 1 and steps:
                            store(sp, k - 1, 1)
                        if not setup and k + 2 <= preps:
                            fetch(k + 2)
                        if k < steps:
                            store(sp, k, 0)
                    if steps:
                        store(sp, steps - 1, 1)
                        sp.wait_ge(stored, 32 * steps)
                    sp.wait_ge(stacked, 192 * preps)

                @block.gpsimd
                def _(pool):
                    chain = [0]

                    def link(ins):
                        chain[0] += 1
                        ins.then_inc(pool_chain, 1)
                        pool.wait_ge(pool_chain, chain[0])

                    if setup:
                        link(nc.gpsimd.memset(ident[:, :], 0.0))
                        nc.gpsimd.affine_select(out=ident[:, :], in_=ident[:, :], compare_op=ALU.not_equal, fill=1.0,
                                                base=0, pattern=[[-1, P]], channel_multiplier=1).then_inc(const, 1)
                        link(nc.gpsimd.memset(minus_half[:, :], -0.5))
                        link(nc.gpsimd.memset(half_mark[:, :], -MARK / 2))
                        link(nc.gpsimd.memset(not_first[:, :], 1.0))
                        link(nc.gpsimd.affine_select(out=not_first[:, 0:1], in_=not_first[:, 0:1],
                                                     compare_op=ALU.is_gt, fill=0.0, base=0, pattern=[[0, 1]],
                                                     channel_multiplier=1))
                        link(nc.gpsimd.memset(ident16[:, :], 0.0))
                        link(nc.gpsimd.affine_select(out=ident16[:, :], in_=ident16[:, :], compare_op=ALU.not_equal,
                                                     fill=1.0, base=0, pattern=[[-1, P]], channel_multiplier=1))
                        link(nc.gpsimd.memset(causal[:, :], 0.0))
                        link(nc.gpsimd.affine_select(out=causal[:, :], in_=causal[:, :], compare_op=ALU.is_ge,
                                                     fill=-BIG, base=0, pattern=[[-1, P]], channel_multiplier=1))
                        link(nc.gpsimd.iota(query[:, :], pattern=[[P, NA]], base=1, channel_multiplier=1,
                                            allow_small_or_imprecise_dtypes=True))
                        link(nc.gpsimd.iota(pad_no[:, :, :], pattern=[[0, NA], [1, PADS]], base=0, channel_multiplier=0,
                                            allow_small_or_imprecise_dtypes=True))
                        nc.gpsimd.memset(va[:, :, :, :], 1.0).then_inc(const, 1)

                    def pool_prepares(n, t):
                        if t == at("root", n):
                            pool.wait_ge(varred, nth(n) + 1)
                            if setup:
                                pool.wait_ge(pool_chain, chain[0])
                            nc.gpsimd.tensor_tensor(rstd[:, :], var[:, :], minus_half[:, :], ALU.pow).then_inc(rooted, 1)
                            pool.wait_ge(rooted, nth(n) + 1)
                            nc.gpsimd.tensor_tensor(shift[:, :], minus_mean[:, :], rstd[:, :], ALU.mult).then_inc(centred, 1)
                        for j in range(2):
                            if t == at(("rest_q", "rest_k")[j], n):
                                wait_read(pool, ("q", "k")[j], n)
                                nc.gpsimd.tensor_tensor(rest[:, j, :], qk32[:, j, :], parts[:, j, 0, :], ALU.subtract)\
                                    .then_inc(rested, 1)
                            if t == at(("third_q", "third_k")[j], n):
                                pool.wait_ge(parted, 2 * nth(n) + j + 1)
                                nc.gpsimd.tensor_tensor(parts[:, j, 2, :], rest[:, j, :], parts[:, j, 1, :],
                                                        ALU.subtract).then_inc(split, 1)
                        for a in range(NA):
                            if t == at(f"s{a}", n):
                                wait_read(pool, f"s{a}", n)
                                edge = s0[:, FOFF[a]:FOFF[a] + P]
                                nc.gpsimd.affine_select(out=edge, in_=edge, compare_op=ALU.is_gt, fill=0.0, base=0,
                                                        pattern=[[1, P]], channel_multiplier=-1).then_inc(ruled, 1)
                            if t == at(f"f{a}", n):
                                wait_read(pool, f"f{a}", n)
                                edge = nf[:, OFF[a] + P * a:OFF[a + 1]]
                                nc.gpsimd.tensor_tensor(edge, edge, causal[:, :], ALU.add).then_inc(nf_done, 1)
                            if t != at(f"mask_{a}", n):
                                continue
                            pool.wait_ge(limited, NA * n + a + 1)
                            edge = work[:, a, PADS + P * a:PADS + P * a + P]
                            link(nc.gpsimd.affine_select(out=edge, in_=edge, compare_op=ALU.not_equal, fill=0.0,
                                                         base=0, pattern=[[-1, P]], channel_multiplier=1))
                            if not setup:
                                pool.wait_ge(masked, NH * NA * n)
                            nc.gpsimd.tensor_tensor(mask[:, into(n), OFF[a]:OFF[a + 1]], nf[:, OFF[a]:OFF[a + 1]],
                                                    work[:, a, PADS:PADS + P * (a + 1)], ALU.subtract)\
                                .then_inc(mask_done, 1)

                    for t in range(end):
                        k, o = divmod(t, NU)
                        if k < steps:
                            a, h0, g = UNITS[o]
                            w = P * (a + 1)
                            for j in range(g):
                                col = ar[:, t % NA_RING, w * j:w * j + w]
                                pool.wait_ge(masked, NH * NA * k + HEADS_TO[o] - g + j + 1)
                                nc.gpsimd.tensor_scalar(col, col, -1.0, mx[:, t % NA_RING, j:j + 1], ALU.mult, ALU.add)\
                                    .then_inc(shifted, 1)
                        for n in range(preps + 1):
                            pool_prepares(n, t)
                        if k < steps:
                            for f in range(NF):
                                if o == dict((n, q) for n, q, _ in FFN_JOBS)[f"h{f}1"] + 1:
                                    wait_read(pool, f"h{f}1", k)
                                    if f == 0 and k >= 1:
                                        wait_full(pool, "down1", k - 1)
                                    nc.gpsimd.tensor_tensor(hsum[:, f, :], h[:, 2 * (f % 2), :], h[:, 2 * (f % 2) + 1, :],
                                                            ALU.add).then_inc(h_sum, 1)

                @block.scalar
                def _(act):
                    chain = [0]

                    def link(ins):
                        chain[0] += 1
                        ins.then_inc(act_chain, 1)

                    def copy(dst, src, name, k, last=True, **kw):
                        ins = nc.scalar.activation(dst, src, ACT.Identity, **kw)
                        ins.then_inc(act_read if last else act_chain, 1)

                    if setup:
                        wait_full(act, "w_attn", 0)
                        m = m_bank("w_attn", 0)
                        copy(wq[:, :].rearrange("c (d h) -> c d h", d=HD), m[:, 0:128].rearrange("c (h d) -> c d h", d=HD),
                             "w_attn", 0, False)
                        copy(wk[:, :].rearrange("c (d h) -> c d h", d=HD),
                             m[:, 128:256].rearrange("c (h d) -> c d h", d=HD), "w_attn", 0, False)
                        copy(wv[:, :], m[:, 256:384], "w_attn", 0)
                        wait_full(act, "w_in", 0)
                        copy(wi_t[:, :], m_bank("w_in", 0)[:, :], "w_in", 0)
                        wait_full(act, "w_out", 0)
                        copy(wo_t[:, :, :].rearrange("p f c -> p (f c)"), m_bank("w_out", 0)[:, :], "w_out", 0)
                        wait_full(act, "lora_b", 0)
                        copy(b_t[:, :], m_bank("lora_b", 0)[:, :], "lora_b", 0)
                        wait_full(act, "small", 0)
                        m = m_bank("small", 0)
                        copy(a_t[:, :], m[:, 0:128], "small", 0, False)
                        copy(wp_t[:, :], m[:, 128:256], "small", 0, False)
                        copy(gate_t[:, :], m[:, 256:264], "small", 0, False)
                        copy(bi_col[:, :], m[:, 264:268], "small", 0, False)
                        copy(bqk_col[:, 0:1], m[:, 268:269], "small", 0, False, scale=SCALE)
                        copy(bqk_col[:, 1:2], m[:, 269:270], "small", 0)
                        wait_full(act, "rows", 0)
                        copy(bias_b[:, :], m_bank("rows", 0)[:, 0:P + NE], "rows", 0)

                    def act_prepares(n, t):
                        if t == at("norm", n):
                            act.wait_ge(centred, nth(n) + 1)
                            if nth(n) >= 1:
                                wait_full(act, "xt", n - 1)
                            for a in range(NA):
                                nc.scalar.activation(xn[:, a, :], xs[:, x_into(n), a, :], ACT.Identity,
                                                     scale=rstd[:, a:a + 1], bias=shift[:, a:a + 1]).then_inc(xn_done, 1)
                        if t == at("choices", n):
                            act.wait_ge(less_done, nth(n) + 1)
                            nc.scalar.activation(expd[:, :, :], less[:, :, :], ACT.Exp).then_inc(exp_done, 1)
                            if n >= 1 and not setup:
                                wait_full(act, "mask1", n - 1)
                            for j in range(2):
                                nc.scalar.activation(
                                    hot_x[:, into(n), j].rearrange("p a (e r) -> p (a e) r", r=R),
                                    hot[:, j].rearrange("p a (e o) -> p (a e) o", o=1).to_broadcast([P, NA * NE, R]),
                                    ACT.Identity).then_inc(hot_wide, 1)
                        for j in range(2):
                            if t == at(("second_q", "second_k")[j], n):
                                act.wait_ge(rested, 2 * nth(n) + j + 1)
                                nc.scalar.activation(parts[:, j, 1, :], rest[:, j, :], ACT.Identity).then_inc(parted, 1)
                        for a in range(NA):
                            if t == at(f"mask_{a}", n):
                                act.wait_ge(selected, n + 1)
                                data = work[:, a, PADS:PADS + P * (a + 1)]
                                nc.scalar.activation(data, data, ACT.Relu, bias=half_mark[:, :])\
                                    .then_inc(limited, 1)
                        r, odd = divmod(t - at("search", n), 2) if n in plan.late else (-1, 0)
                        if 0 <= r < HALVINGS and not odd:
                            act.wait_ge(halved, (HALVINGS + 1) * n + r + 1)
                            if r == 0:
                                act.wait_ge(nf_done, NA * (n + 1))
                            for a in (2, 3):
                                nc.scalar.activation(junk[:, a - 2, 0:P * (a + 1)], nf[:, OFF[a]:OFF[a + 1]], ACT.Sign,
                                                     bias=cut[:, a:a + 1], scale=-1.0, accum_out=above[:, a:a + 1])\
                                    .then_inc(counted, 1)

                    for t in range(end):
                        k, o = divmod(t, NU)
                        for name, n in plan.at.get(t, []):
                            if plan.reads[name, n][0] != "act":
                                continue
                            wait_full(act, name, n)
                            m = m_bank(name, n)
                            if name == "xt":
                                if n >= 1 and not setup:
                                    wait_full(act, f"h{NF - 1}1", n - 1)
                                copy(xnt[:, into(n), :], m[:, :], name, n)
                            elif name in ("q", "k"):
                                j = ("q", "k").index(name)
                                if nth(n) >= 1:
                                    act.wait_ge(split, 2 * nth(n))
                                if n >= 1:
                                    act.wait_ge(stacked, 192 * n)
                                if setup:
                                    wait_read(act, "small", 0)
                                copy(qk32[:, j, :], m[:, :], name, n, False, bias=bqk_col[:, j:j + 1],
                                     scale=(SCALE, 1.0)[j])
                                copy(parts[:, j, 0, :], m[:, :], name, n, bias=bqk_col[:, j:j + 1],
                                     scale=(SCALE, 1.0)[j])
                            elif name[0] == "s":
                                j = int(name[1])
                                if n >= 1:
                                    act.wait_ge(scanned, NA * (n - 1) + j + 1)
                                if setup:
                                    act.wait_ge(const, 2)
                                w = T - P * j
                                nc.scalar.activation(s0[:, FOFF[j]:FOFF[j] + w], m[:, 0:w], ACT.Relu,
                                                     scale=not_first[:, min(j, 1):min(j, 1) + 1]).then_inc(act_read, 1)
                            elif name == "z":
                                if n >= 1:
                                    wait_read(act, "mask1", n - 1)
                                copy(z[:, :], m[:, :], name, n)
                            elif name[0] == "h":
                                f, j = int(name[1]), int(name[2])
                                if NF * n + f >= 2:
                                    act.wait_ge(h_sum, NF * n + f - 1)
                                nc.scalar.activation(h[:, 2 * (f % 2) + j, :], m[:, :], ACT.Relu, bias=bi_col[:, f:f + 1])\
                                    .then_inc(act_read, 1)
                            elif name[0:2] == "yt":
                                a = int(name[2])
                                if n >= 1 and a in (0, 3):
                                    wait_full(act, ("proj0", "proj1")[a == 3], n - 1)
                                copy(yt[:, a, :], m[:, 0:P], name, n)
                        u = t - LAG_T
                        if 0 <= u < NU * steps:
                            a, h0, g = UNITS[u % NU]
                            act.wait_ge(turned, u + 1)
                            if u >= NP_RING:
                                act.wait_ge(summed, u - NP_RING + 1)
                            w = P * (a + 1) * g
                            nc.scalar.activation(pr[:, u % NP_RING, 0:w], ps_t[u % NT_RING][:, 0:w], ACT.Exp, scale=-1.0)\
                                .then_inc(weighed, 1)
                        for n in range(preps + 1):
                            act_prepares(n, t)

                @block.tensor
                def _(pe):
                    def fill(name, n):
                        i_place = plan.place[name, n]
                        if i_place >= NM_RING:
                            wait_read(pe, *plan.last[i_place - NM_RING])
                        m = m_bank(name, n)
                        c = into(n)
                        if name == "w_attn":
                            pe.wait_ge(w_in, 16 * 16)
                            pe.wait_ge(const, 1)
                            for j in range(3):
                                last = nc.tensor.transpose(m[:, P * j:P * j + P], raw_attn[:, j, :], ident[:, :])
                        elif name == "w_in":
                            for f in range(NF):
                                last = nc.tensor.transpose(m[:, P * f:P * f + P], raw_wi[:, f, :], ident[:, :])
                        elif name == "w_out":
                            for f in range(NF):
                                last = nc.tensor.transpose(m[:, P * f:P * f + P], raw_wo[:, P * f:P * f + P], ident[:, :])
                        elif name == "lora_b":
                            for f in range(NF):
                                last = nc.tensor.transpose(m[:, P * f:P * f + P],
                                                           raw_b[:, f].rearrange("p e r -> p (e r)"), ident[:, :])
                        elif name == "small":
                            nc.tensor.transpose(m[:, 0:P], raw_a, ident[:, :])
                            nc.tensor.transpose(m[:, P:2 * P], raw_wp, ident[:, :])
                            nc.tensor.transpose(m[:, 256:264], raw_gate[:, :], ident[0:NE, 0:NE])
                            nc.tensor.transpose(m[:, 264:268], raw_bi[:, :], ident[0:NF, 0:NF])
                            pe.wait_ge(w_prep, 3)
                            last = nc.tensor.transpose(m[:, 268:270], bqk_dh[:, :], ident[0:2, 0:2])
                        elif name == "rows":
                            last = nc.tensor.matmul(m[:, 0:P + NE], ones[0:1, 0:P], bias_row[:, :], start=True, stop=True)
                        elif name == "xt":
                            pe.wait_ge(xn_done, NA * (nth(n) + 1))
                            for a in range(NA):
                                last = nc.tensor.transpose(m[:, P * a:P * a + P], xn[:, a, :], ident[:, :])
                        elif name in ("q", "k"):
                            wait_read(pe, "xt", n)
                            last = nc.tensor.matmul(m[:, :], (wq if name == "q" else wk)[:, :], xnt[:, c, :],
                                                    start=True, stop=True)
                        elif name == "v":
                            for a in range(NA):
                                last = nc.tensor.matmul(m[:, P * a:P * a + P], xnt[:, c, P * a:P * a + P], wv[:, :],
                                                        start=True, stop=True)
                        elif name == "gate":
                            if setup:
                                wait_read(pe, "small", 0)
                            for a in range(NA):
                                last = nc.tensor.matmul(m[:, NE * a:NE * a + NE], xnt[:, c, P * a:P * a + P], gate_t[:, :],
                                                        start=True, stop=True)
                        elif name[0] == "s":
                            j = int(name[1])
                            pe.wait_ge(stacked, 192 * (n + 1))
                            last = nc.tensor.matmul(m[:, 0:T - P * j], ks[:, c, 0, P * j:P * j + P], qs[:, c, 0, P * j:T],
                                                    start=True, stop=True)
                        elif name == "flag":
                            pe.wait_ge(sel, n + 1)
                            last = nc.tensor.matmul(m[0:1, 0:NA], ones[:, 0:1], bad[:, 0, :], start=True, stop=True)
                        elif name[0] == "f":
                            a = int(name[1])
                            pe.wait_ge(scanned, NA * (n + 1))
                            for j in range(a + 1):
                                at = FOFF[j] + P * (a - j)
                                last = nc.tensor.transpose(m[:, P * j:P * j + P], ft[:, at:at + P], ident[:, :])
                        elif name == "z":
                            last = nc.tensor.matmul(m[:, :], a_t[:, :], xnt[:, n % 2, :], start=True, stop=True)
                        elif name[0:4] == "mask":
                            j = int(name[4])
                            for a in range(NA):
                                last = nc.tensor.matmul(m[:, P * a:P * a + P], hot_x[:, n % 2, j, a, :], ident16[:, :],
                                                        start=True, stop=True)
                        elif name[0] == "h":
                            f, j = int(name[1]), int(name[2])
                            wait_read(pe, f"mask{j}", n)
                            if j == 0:
                                nc.tensor.matmul(m[:, :], wi_t[:, P * f:P * f + P], xnt[:, n % 2, :], start=True, stop=False)
                            else:
                                wait_read(pe, f"h{f}0", n)
                            last = nc.tensor.matmul(m[:, :], b_t[:, P * f:P * f + P], zm[:, j, :], start=False, stop=True,
                                                    skip_group_check=(j == 1))
                        elif name[0:4] == "down":
                            pe.wait_ge(h_sum, NF * (n + 1))
                            for a in HALF[int(name[4])]:
                                for f in range(NF):
                                    nc.tensor.matmul(m[:, P * a:P * a + P], hsum[:, f, P * a:P * a + P], wo_t[:, f, :],
                                                     start=(f == 0), stop=False)
                                last = nc.tensor.matmul(m[:, P * a:P * a + P], ones[0:1, 0:P], bo2_row[:, :],
                                                        start=False, stop=True)
                        elif name[0:2] == "yt":
                            a = int(name[2])
                            pe.wait_ge(normed, NA * n + a + 1)
                            last = nc.tensor.transpose(m[:, 0:P], y[:, a, :, :].rearrange("p h d -> p (h d)"), ident[:, :])
                        elif name[0:4] == "proj":
                            lo, hi = ((0, NA - 1), (NA - 1, NA))[int(name[4])]
                            wait_read(pe, f"yt{hi - 1}", n)
                            for a in range(lo, hi):
                                at = P * (a - lo)
                                nc.tensor.matmul(m[:, at:at + P], yt[:, a, :], wp_t[:, :], start=True, stop=False)
                                last = nc.tensor.matmul(m[:, at:at + P], ones[0:1, 0:P], bp_row[:, :],
                                                        start=False, stop=True)
                        last.then_inc(m_full, 1)

                    def score(u):
                        k, o = divmod(u, NU)
                        a, h0, g = UNITS[o]
                        w = P * (a + 1)
                        if o == 0 and k >= 1:
                            pe.wait_ge(stacked, 192 * k)
                        if u >= NS_RING:
                            kk, oo = divmod(u - NS_RING, NU)
                            pe.wait_ge(masked, NH * NA * kk + HEADS_TO[oo])
                        for j in range(g):
                            last = nc.tensor.matmul(ps_s[u % NS_RING][:, w * j:w * j + w], qs[:, k % 2, h0 + j, P * a:P * a + P],
                                                    ks[:, k % 2, h0 + j, 0:w], start=True, stop=True)
                        last.then_inc(scored, 1)

                    def turn(u):
                        k, o = divmod(u, NU)
                        a, h0, g = UNITS[o]
                        pe.wait_ge(shifted, NH * NA * k + HEADS_TO[o])
                        if u >= NT_RING:
                            pe.wait_ge(weighed, u - NT_RING + 1)
                        for j in range(g * (a + 1)):
                            last = nc.tensor.transpose(ps_t[u % NT_RING][:, P * j:P * j + P],
                                                       ar[:, u % NA_RING, P * j:P * j + P], ident[:, :])
                        last.then_inc(turned, 1)

                    def weigh(u):
                        k, o = divmod(u, NU)
                        a, h0, g = UNITS[o]
                        pe.wait_ge(weighed, u + 1)
                        if h0 == 0 and NA * k + a >= 1:
                            pe.wait_ge(normed, NA * k + a)
                        for j in range(g):
                            hh = h0 + j
                            wide = MOVED if hh < NH - 1 else OW
                            for c in range(a + 1):
                                at = P * ((a + 1) * j + c)
                                last = nc.tensor.matmul(ps_o[:, OW * hh:OW * hh + wide], pr[:, u % NP_RING, at:at + P],
                                                        va[:, k % 2, c, VW * hh:VW * hh + wide], start=(c == 0), stop=(c == a))
                        last.then_inc(summed, 1)

                    if setup:
                        for name in SETUP_JOBS:
                            fill(name, 0)
                    for t in range(end):
                        for name, n in plan.at.get(t, []):
                            fill(name, n)
                        if t < NU * steps:
                            score(t)
                        if 0 <= t - LAG_T < NU * steps:
                            turn(t - LAG_T)
                        if 0 <= t - LAG_P < NU * steps:
                            weigh(t - LAG_P)

                @block.vector
                def _(dve):
                    chain = [0]

                    def link(ins):
                        chain[0] += 1
                        ins.then_inc(dve_chain, 1)
                        dve.wait_ge(dve_chain, chain[0])

                    if setup:
                        for stack in (qs, ks):
                            nc.vector.memset(stack[:, 0].rearrange("p h t -> p (h t)").bitcast(F32), 0.0)\
                                .then_inc(zeroed, 1)
                        nc.vector.memset(ones[:, :], 1.0).then_inc(w_prep, 1)
                        for e in range(NE):
                            link(nc.vector.memset(rank[:, :, e:e + 1], float(NE - e)))
                        dve.wait_ge(w_in, 16 * 16)
                        nc.vector.tensor_copy(bqk_dh[:, :].rearrange("t (d h) -> t d h", d=HD),
                                              raw_bqk[:, :].rearrange("t (h d) -> t d h", d=HD)).then_inc(w_prep, 1)
                        nc.vector.tensor_scalar(bo2_row[:, :], bo_row[:, :], 2.0, None, ALU.mult).then_inc(w_prep, 1)

                    def constants():
                        for stack in (qs, ks):
                            nc.vector.memset(stack[:, 1].rearrange("p h t -> p (h t)").bitcast(F32), 0.0)\
                                .then_inc(zeroed, 1)
                        dve.wait_ge(const, 2)
                        link(nc.vector.reciprocal(reach[:, :], query[:, :]))
                        link(nc.vector.tensor_scalar(reach[:, :], reach[:, :], REACH * KEEP, 1.0, ALU.mult, ALU.min))
                        link(nc.vector.tensor_scalar(all_low[:, :], query[:, :], KEEP + 0.5, None, ALU.is_lt))
                        for a in range(NA):
                            w = P * (a + 1)
                            link(nc.vector.memset(few[:, a:a + 1], float(w - AIM if a < 2 else w - 2 * AIM)))

                    def moments(n):
                        c = into(n)
                        dve.wait_ge(x_in, 16 * (nth(n) + 1))
                        if nth(n) >= 1:
                            dve.wait_ge(centred, nth(n))
                        for a in range(NA):
                            last = nc.vector.bn_stats(stats[:, a, :], xs[:, x_into(n), a, :])
                            last.then_inc(dve_chain, 1)
                            chain[0] += 1
                        dve.wait_ge(dve_chain, chain[0])
                        for a in range(NA):
                            nc.vector.bn_aggr(mv[:, a, :], stats[:, a, :]).then_inc(dve_chain, 1)
                            chain[0] += 1
                        dve.wait_ge(dve_chain, chain[0])
                        link(nc.vector.tensor_scalar(minus_mean[:, :], mv[:, :, 0], -1.0, None, ALU.mult))
                        nc.vector.tensor_scalar(var[:, :], mv[:, :, 1], EPS, None, ALU.add).then_inc(varred, 1)

                    def wide(col):
                        return col.rearrange("p (a o) -> p a o", o=1).to_broadcast([P, NA, NE])

                    def choose(j):
                        link(nc.vector.tensor_reduce(best[:, j, :], logit[:, :, :], AX, ALU.max))
                        link(nc.vector.tensor_tensor(eq[:, :, :], logit[:, :, :], wide(best[:, j, :]), ALU.is_equal))
                        link(nc.vector.tensor_tensor(tie[:, :, :], eq[:, :, :], rank[:, :, :], ALU.mult))
                        link(nc.vector.tensor_reduce(best[:, 2 + j, :], tie[:, :, :], AX, ALU.max))
                        ins = nc.vector.tensor_tensor(hot[:, j], tie[:, :, :], wide(best[:, 2 + j, :]), ALU.is_equal)
                        return ins

                    def route(n):
                        wait_full(dve, "gate", n)
                        if setup:
                            wait_read(dve, "rows", 0)
                        if nth(n) >= 1:
                            dve.wait_ge(hot_wide, 2 * nth(n))
                        m = m_bank("gate", n)
                        nc.vector.tensor_tensor(
                            logit[:, :, :], m[:, 0:NA * NE].rearrange("p (a e) -> p a e", e=NE),
                            bias_b[:, P:P + NE].rearrange("p (o e) -> p o e", o=1).to_broadcast([P, NA, NE]), ALU.add)\
                            .then_inc(dve_read, 1)
                        dve.wait_ge(dve_read, plan.reads["gate", n][1])
                        link(choose(0))

                    def route_second(n):
                        link(nc.vector.tensor_tensor(less[:, :, 0:NE], logit[:, :, :], wide(best[:, 0, :]), ALU.subtract))
                        link(nc.vector.tensor_scalar(eq[:, :, :], hot[:, 0], -BIG, None, ALU.mult))
                        link(nc.vector.tensor_tensor(logit[:, :, :], logit[:, :, :], eq[:, :, :], ALU.add))
                        link(choose(1))
                        link(nc.vector.tensor_tensor(hot[:, 1], hot[:, 1], hot[:, 0], ALU.subtract))
                        nc.vector.tensor_tensor(less[:, :, NE:NE + 1].rearrange("p a o -> p (a o)"), best[:, 1, :],
                                                best[:, 0, :], ALU.subtract).then_inc(less_done, 1)

                    def share(n):
                        dve.wait_ge(exp_done, nth(n) + 1)
                        link(nc.vector.tensor_reduce(den[:, :], expd[:, :, 0:NE], AX, ALU.add))
                        link(nc.vector.reciprocal(den[:, :], den[:, :]))
                        c = into(n)
                        link(nc.vector.tensor_scalar(vsum[:, c, :], expd[:, :, NE:NE + 1].rearrange("p a o -> p (a o)"),
                                                     1.0, None, ALU.add))
                        link(nc.vector.tensor_tensor(vsum[:, c, :], vsum[:, c, :], den[:, :], ALU.mult))

                    def forget(n, j):
                        if j == 0 and n >= 1:
                            wait_full(dve, f"f{NA - 1}", n - 1)
                        w = T - P * j
                        link(nc.vector.memset(ft[:, FOFF[j]:FOFF[j] + 1], 0.0))
                        dve.wait_ge(ruled, NA * n + j + 1)
                        nc.vector.tensor_tensor_scan(ft[:, FOFF[j] + 1:FOFF[j] + w], ones[:, 0:w - 1],
                                                     s0[:, FOFF[j]:FOFF[j] + w - 1], 0.0, ALU.mult, ALU.add)\
                            .then_inc(scanned, 1)

                    def search_start(n):
                        dve.wait_ge(dve_read, plan.reads[f"f{NA - 1}", n][1])
                        link(nc.vector.tensor_tensor(step_to[:, :], greatest[:, :], reach[:, :], ALU.mult))
                        for r in range(HALVINGS):
                            link(nc.vector.tensor_scalar(halves[:, r, :], step_to[:, :], 0.5 ** (r + 1), None, ALU.mult))
                        nc.vector.tensor_copy(cut[:, :], halves[:, 0, :]).then_inc(halved, 1)

                    def search_count(n, r):
                        dve.wait_ge(halved, (HALVINGS + 1) * n + r + 1)
                        if r == 0:
                            dve.wait_ge(nf_done, NA * (n + 1))
                            if n >= 1:
                                dve.wait_ge(mask_done, NA * n)
                        for a in (0, 1):
                            w = P * (a + 1)
                            chain[0] += 1
                            nc.vector.tensor_scalar(work[:, a, PADS:PADS + w], nf[:, OFF[a]:OFF[a + 1]], cut[:, a:a + 1],
                                                    None, ALU.is_lt, ALU.add, accum_out=above[:, a:a + 1])\
                                .then_inc(dve_chain, 1)

                    def search_step(n, r):
                        dve.wait_ge(dve_chain, chain[0])
                        dve.wait_ge(counted, 2 * HALVINGS * n + 2 * (r + 1))
                        link(nc.vector.tensor_tensor(step_to[:, :], above[:, :], few[:, :], ALU.is_ge))
                        link(nc.vector.scalar_tensor_tensor(out=step_to[:, :], in0=step_to[:, :], scalar=-0.5,
                                                            in1=halves[:, r, :], op0=ALU.add, op1=ALU.mult))
                        nc.vector.tensor_tensor(cut[:, :], cut[:, :], step_to[:, :], ALU.add).then_inc(halved, 1)

                    def under_threshold(n, tiles):
                        if 0 in tiles:
                            dve.wait_ge(halved, (HALVINGS + 1) * (n + 1))
                            link(nc.vector.scalar_tensor_tensor(out=cut[:, :], in0=all_low[:, :], scalar=-BIG / 10,
                                                                in1=cut[:, :], op0=ALU.mult, op1=ALU.add))
                        for a in tiles:
                            chain[0] += 1
                            nc.vector.tensor_scalar(work[:, a, PADS:PADS + P * (a + 1)], nf[:, OFF[a]:OFF[a + 1]],
                                                    cut[:, a:a + 1], None, ALU.is_ge, ALU.add,
                                                    accum_out=count[:, a:a + 1]).then_inc(dve_chain, 1)

                    def in_reach():
                        dve.wait_ge(dve_chain, chain[0])
                        link(nc.vector.tensor_scalar(bad[:, 0, :], count[:, :], KEEP + 0.5, None, ALU.is_gt))
                        link(nc.vector.scalar_tensor_tensor(out=bad[:, 1, :], in0=all_low[:, :], scalar=1000.0,
                                                            in1=count[:, :], op0=ALU.mult, op1=ALU.add))
                        link(nc.vector.tensor_scalar(bad[:, 1, :], bad[:, 1, :], KEEP - SLACK - 0.5, None, ALU.is_lt))
                        nc.vector.tensor_tensor(bad[:, 0, :], bad[:, 0, :], bad[:, 1, :], ALU.add).then_inc(sel, 1)
                        link(nc.vector.tensor_scalar(count[:, :], count[:, :], SLACK - KEEP, None, ALU.add))
                        link(nc.vector.tensor_tensor(pads01[:, :, :], pad_no[:, :, :],
                                                     count[:, :].rearrange("p (a o) -> p a o", o=1)
                                                     .to_broadcast([P, NA, PADS]), ALU.is_lt))
                        link(nc.vector.tensor_scalar(work[:, :, 0:PADS], pads01[:, :, :], 3.1e38, MARK, ALU.mult, ALU.add))

                    def marks(tiles):
                        for a in tiles:
                            chain[0] += 1
                            data = work[:, a, PADS:PADS + P * (a + 1)]
                            nc.vector.scalar_tensor_tensor(out=data, in0=data, scalar=MARK, in1=nf[:, OFF[a]:OFF[a + 1]],
                                                           op0=ALU.mult, op1=ALU.add).then_inc(dve_chain, 1)
                        dve.wait_ge(dve_chain, chain[0])

                    def eight_largest(tiles):
                        dve.wait_ge(dve_chain, chain[0])
                        for a in tiles:
                            chain[0] += 1
                            nc.vector.max(top8[:, a, :], work[:, a, 0:PADS + P * (a + 1)]).then_inc(dve_chain, 1)

                    def replace_largest(tiles):
                        dve.wait_ge(dve_chain, chain[0])
                        for a in tiles:
                            chain[0] += 1
                            row = work[:, a, 0:PADS + P * (a + 1)]
                            nc.vector.match_replace(row, top8[:, a, :], row, MARK).then_inc(dve_chain, 1)

                    def rounds_from_scratch(n):
                        wait_full(dve, "flag", n)
                        nc.vector.tensor_reduce(flag[:, :], m_bank("flag", n)[0:1, 0:NA], AX, ALU.add).then_inc(dve_read, 1)
                        dve.wait_ge(dve_read, plan.reads["flag", n][1])
                        dve.wait_ge(dve_chain, chain[0])
                        link(nc.vector.tensor_copy(flag_i[:, :], flag[:, :]))
                        failed = dve.value_load(flag_i[0:1, 0:1])
                        with dve.If(failed > 0):
                            dve.sem_clear(again)
                            nc.vector.memset(work[:, :, 0:PADS], MARK).then_inc(again, 1)
                            dve.wait_ge(again, 1)
                            nc.vector.memset(work[:, :, 0:8 * ROUNDS - KEEP], 1.0e37).then_inc(again, 1)
                            for a in range(NA):
                                nc.vector.tensor_copy(work[:, a, PADS:PADS + P * (a + 1)], nf[:, OFF[a]:OFF[a + 1]])\
                                    .then_inc(again, 1)
                            dve.wait_ge(again, 2 + NA)
                            with dve.Fori(0, ROUNDS):
                                dve.sem_clear(again)
                                for a in range(NA):
                                    nc.vector.max(top8[:, a, :], work[:, a, 0:PADS + P * (a + 1)]).then_inc(again, 1)
                                for a in range(NA):
                                    dve.wait_ge(again, a + 1)
                                    row = work[:, a, 0:PADS + P * (a + 1)]
                                    nc.vector.match_replace(row, top8[:, a, :], row, MARK).then_inc(again, 1)
                                dve.wait_ge(again, 2 * NA)
                        nc.vector.memset(flag[:, :], 0.0).then_inc(selected, 1)

                    for t in range(end):
                        k, o = divmod(t, NU)
                        for name, n in plan.at.get(t, []):
                            if plan.reads[name, n][0] != "dve":
                                continue
                            m = m_bank(name, n)
                            if name == "v":
                                wait_full(dve, name, n)
                                if setup:
                                    wait_read(dve, "rows", 0)
                                    dve.wait_ge(const, 2)
                                elif n >= 1:
                                    dve.wait_ge(summed, NU * n)
                                for a in range(NA):
                                    ins = nc.vector.tensor_tensor(
                                        va[:, into(n), a, 0:NH * VW].rearrange("p (h d) -> p h d", d=VW)[:, :, 0:HD],
                                        m[:, P * a:P * a + P].rearrange("p (h d) -> p h d", d=HD),
                                        bias_b[:, 0:P].rearrange("p (h d) -> p h d", d=HD), ALU.add)
                                ins.then_inc(dve_read, 1)
                            elif name == "gate":
                                route(n)
                            elif name == "flag":
                                rounds_from_scratch(n)
                            elif name[0] == "f":
                                a = int(name[1])
                                wait_full(dve, name, n)
                                if n >= 1 and a == 0:
                                    dve.wait_ge(mask_done, NA * n)
                                nc.vector.tensor_scalar(nf[:, OFF[a]:OFF[a + 1]], m[:, 0:P * (a + 1)], -1.0, None,
                                                        ALU.mult, ALU.min, accum_out=greatest[:, a:a + 1])\
                                    .then_inc(dve_read, 1)
                            elif name[0:4] == "mask":
                                j = int(name[4])
                                wait_full(dve, name, n)
                                wait_read(dve, "z", n)
                                if n >= 1:
                                    wait_full(dve, f"h{NF - 1}1", n - 1)
                                nc.vector.tensor_tensor(zm[:, j, :], m[:, :], z[:, :], ALU.mult).then_inc(dve_read, 1)
                            elif name[0:4] == "down":
                                wait_full(dve, name, n)
                                for a in HALF[int(name[4])]:
                                    ins = nc.vector.scalar_tensor_tensor(
                                        out=down[:, a, :], in0=m[:, P * a:P * a + P], scalar=vsum[:, n % 2, a:a + 1],
                                        in1=xs[:, n % XN, a, :], op0=ALU.mult, op1=ALU.add)
                                ins.then_inc(dve_read, 1)
                            elif name[0:4] == "proj":
                                lo, hi = ((0, NA - 1), (NA - 1, NA))[int(name[4])]
                                wait_full(dve, name, n)
                                wait_read(dve, "down1", n)
                                if n >= 1:
                                    dve.wait_ge(stored, 32 * n)
                                nc.vector.tensor_tensor(res[:, lo:hi, :].rearrange("p a c -> p (a c)"),
                                                        m[:, 0:P * (hi - lo)],
                                                        down[:, lo:hi, :].rearrange("p a c -> p (a c)"), ALU.add)\
                                    .then_inc(dve_read, 1)
                        if k < steps:
                            a, h0, g = UNITS[o]
                            w = P * (a + 1)
                            dve.wait_ge(scored, t + 1)
                            if t >= NA_RING:
                                dve.wait_ge(turned, t - NA_RING + 1)
                            if h0 == 0 and k >= 1:
                                dve.wait_ge(mask_done, NA * (k - 1) + a + 1)
                            for j in range(g):
                                nc.vector.tensor_tensor_reduce(
                                    out=ar[:, t % NA_RING, w * j:w * j + w], in0=ps_s[t % NS_RING][:, w * j:w * j + w],
                                    in1=mask[:, k % 2, OFF[a]:OFF[a + 1]], scale=1.0, scalar=MARK, op0=ALU.add, op1=ALU.max,
                                    accum_out=mx[:, t % NA_RING, j:j + 1]).then_inc(masked, 1)
                        for kk in range(steps):
                            for a in range(NA):
                                if t == NU * kk + LAST[a] + LAG_P:
                                    dve.wait_ge(summed, NU * kk + LAST[a] + 1)
                                    if kk >= 1:
                                        wait_full(dve, f"yt{a}", kk - 1)
                                    o3 = ps_o[:, :].rearrange("p (h d) -> p h d", d=OW)
                                    link(nc.vector.reciprocal(rec[:, :].rearrange("p (h o) -> p h o", o=1),
                                                              o3[:, :, HD:VW]))
                                    nc.vector.tensor_tensor(
                                        y[:, a, :, :], o3[:, :, 0:HD],
                                        rec[:, :].rearrange("p (h o) -> p h o", o=1).to_broadcast([P, NH, HD]), ALU.mult)\
                                        .then_inc(normed, 1)
                        for n in range(preps + 1):
                            if t == at("moments", n):
                                moments(n)
                                if setup and n == 0:
                                    constants()
                            if t == at("route", n):
                                route_second(n)
                            if t == at("share", n):
                                share(n)
                            for c in range(NA):
                                if t == at(f"scan{c}", n):
                                    forget(n, c)
                            if n not in plan.late:
                                continue
                            if t == at("search", n) - 1:
                                search_start(n)
                            r, odd = divmod(t - at("search", n), 2)
                            if 0 <= r < HALVINGS:
                                (search_step if odd else search_count)(n, r)
                            for width, tiles in (("narrow", (0, 1, 2)), ("wide", (3,))):
                                if t == at(f"under_{width}", n):
                                    under_threshold(n, tiles)
                            if t == at("reach", n):
                                in_reach()
                            for width, tiles in (("narrow", (0, 1, 2)), ("wide", (3,))):
                                if t == at(f"marks_{width}", n):
                                    marks(tiles)
                            for r in range(FAST):
                                for width, tiles in (("narrow", (0, 1)), ("wide", (2, 3))):
                                    if t == at(f"top{r}_{width}", n):
                                        eight_largest(tiles)
                                for width, tiles in (("narrow", (0, 1, 2)), ("wide", (3,))):
                                    if t == at(f"replace{r}_{width}", n):
                                        replace_largest(tiles)

            with nc.Block() as clear:
                @clear.sync
                def _(sp):
                    for one in s.values():
                        sp.sem_clear(one)

        run_block(0, 0, 1, setup=True)
        with nc.Fori(0, B // STEPS) as i:
            run_block(i, STEPS, STEPS)


_INS = ['L0_attn_x', 'L0_attn_w_attn', 'L0_attn_b_attn', 'L0_attn_w_proj', 'L0_attn_b_proj', 'L0_ffn_wi', 'L0_ffn_bi',
        'L0_ffn_wo', 'L0_ffn_bo', 'L0_ffn_lora_A', 'L0_ffn_lora_B', 'L0_ffn_gate_w', 'L0_ffn_gate_b']


def kernel(**inputs):
    import numpy as _np
    import concourse.bacc as _bacc
    from concourse import mybir as _mybir
    from concourse.bass_utils import run_bass_kernel_spmd as _run
    nc = _bacc.Bacc("TRN2", target_bir_lowering=False, num_devices=1)
    arrays, args = {}, []
    for name in _INS:
        a = _np.ascontiguousarray(inputs[name])
        arrays[f"in_{name}"] = a
        args.append(nc.dram_tensor(f"in_{name}", a.shape, _mybir.dt.from_np(a.dtype), kind="ExternalInput").ap())
    out = nc.dram_tensor("out", (8, 512, 128), _mybir.dt.float32, kind="ExternalOutput").ap()
    build(nc, *args, out)
    r = _run(nc, [arrays], core_ids=[0])
    return r.results[0]["out"]
```

```python
from contextlib import ExitStack

import concourse.bass as bass
from concourse import mybir

F32 = mybir.dt.float32
BF16 = mybir.dt.bfloat16
ALU = mybir.AluOpType
ACT = mybir.ActivationFunctionType
AX = mybir.AxisListType.X

P = 128
B, T, C = 8, 512, 128
XN = 4
STEPS = 4
NH, HD = 16, 8
NA = T // P
HALF = ((0, 1), (2, 3))
FF, NE, R = 512, 8, 16
NF = FF // P
KEEP = max(1, int(T * 0.2)) - 1
SCALE = 1.0 / HD ** 0.5
EPS = 1e-5
BIG = 1.0e30
MARK = -3.0e38
FAST = 2
SLACK = 8 * FAST
HALVINGS = 8
REACH = 1.25
AIM = KEEP - SLACK / 2 + 0.5
PADS = SLACK
ROUNDS = -(-KEEP // 8)
WIDE = PADS + T
VW = HD + 1
OW = 512 // NH

Q_PART = (0, 0, 1, 1, 0, 2)
K_PART = (0, 1, 0, 1, 2, 0)
ROWS = 96

UNITS = [(a, h, 4 // w) for a, w in ((0, 1), (1, 2), (2, 4), (3, 4)) for h in range(0, NH, 4 // w)]
NU = len(UNITS)
LAST = [max(u for u in range(NU) if UNITS[u][0] == a) for a in range(NA)]
HEADS_TO = [sum(x[2] for x in UNITS[:u + 1]) for u in range(NU)]
OFF = [P * a * (a + 1) // 2 for a in range(NA + 1)]
FOFF = [sum(T - P * x for x in range(c)) for c in range(NA + 1)]

NS_RING, NT_RING, NM_RING = 3, 2, 2
NA_RING, NP_RING = 6, 4
LAG_T, LAG_P = 3, 6
YT_LAG = 3
TAIL = 12

HIDDEN_AT = (14, 17, 20, 23)
FFN_JOBS = [("z", 1, "act"), ("mask0", 3, "dve"), ("mask1", 4, "dve")] + \
    [(f"h{f}{j}", HIDDEN_AT[f] + j, "act") for f in range(NF) for j in range(2)] + \
    [("down0", 28, "dve"), ("down1", 30, "dve")]
ATT_JOBS = [(f"yt{a}", LAST[a] + LAG_P + YT_LAG, "act") for a in range(NA)] + \
    [("proj0", 40, "dve"), ("proj1", LAST[3] + LAG_P + YT_LAG + 2, "dve")]
PREP_AT = {
    "moments": (0, -18), "root": (0, -17), "norm": (1, -15), "xt": (2, -12), "q": (3, -10), "k": (4, -8),
    "rest_q": (4, -9), "second_q": (5, -8), "third_q": (6, -7),
    "rest_k": (5, -7), "second_k": (6, -6), "third_k": (7, -5),
    "gate": (8, -1), "route": (8, 1), "choices": (9, 3), "share": (10, 4),
    "s0": (13, 5), "s1": (14, 6), "s2": (15, 7), "s3": (16, 8), "v": (17, 9),
    "scan0": (14, 6), "scan1": (15, 7), "scan2": (16, 8), "scan3": (17, 9),
    "f0": (18, 10), "f1": (19, 11), "f2": (20, 12), "f3": (21, 13),
    "search": (22, 14),
    "under_narrow": (38, 30), "under_wide": (38, 30), "reach": (38, 31),
    "marks_narrow": (38, 34), "marks_wide": (38, 34),
    "top0_narrow": (39, 35), "top0_wide": (39, 35), "replace0_narrow": (39, 36), "replace0_wide": (39, 37),
    "top1_narrow": (39, 37), "top1_wide": (39, 38), "replace1_narrow": (39, 39), "replace1_wide": (39, 40),
    "flag": (40, 41),
    "mask_0": (40, 42), "mask_1": (40, 45), "mask_2": (40, 48), "mask_3": (40, 50),
}
SECOND_AT = {
    "moments": 23, "root": 23, "norm": 24, "xt": 26, "q": 27, "k": 29, "gate": 30, "route": 31, "choices": 32,
    "share": 34, "rest_q": 28, "second_q": 29, "third_q": 30, "rest_k": 30, "second_k": 31, "third_k": 32,
}
PREP_JOBS = [("xt", "act"), ("q", "act"), ("k", "act"), ("gate", "dve"), ("v", "dve")] + \
    [(f"s{c}", "act") for c in range(NA)] + [(f"f{a}", "dve") for a in range(NA)] + [("flag", "dve")]

EARLY = ("moments", "root", "norm", "xt", "q", "k", "rest_q", "second_q", "third_q", "rest_k", "second_k", "third_k",
         "gate", "route", "choices", "share")

NW = 14
SETUP_JOBS = [("w_attn", 0), ("small", 7), ("rows", 7), ("w_in", 12), ("w_out", 12), ("lora_b", 12)]


class Plan:

    def __init__(self, steps, preps, setup):
        self.setup = setup
        self.late = range(preps)
        self.early = range(0 if setup else 1, preps + 1)
        jobs = [(o, (name, 0), "act") for name, o in SETUP_JOBS] if setup else []
        for k in range(steps):
            jobs += [(NU * k + o, (name, k), who) for name, o, who in FFN_JOBS + ATT_JOBS]
        jobs += [(self.slot(name, n), (name, n), who) for name, who in PREP_JOBS
                 for n in (self.early if name in EARLY else self.late)]
        jobs.sort(key=lambda x: x[0])
        self.at, self.number, self.place, self.reads, self.last = {}, {}, {}, {}, []
        counts = {"act": 0, "dve": 0}
        for i, (t, key, who) in enumerate(jobs):
            self.at.setdefault(t, []).append(key)
            self.number[key] = i
            if key[0][0] == "h" and key[0][2] == "1":
                self.place[key] = self.place[key[0][:2] + "0", key[1]]
                self.last[self.place[key]] = key
            else:
                self.place[key] = len(self.last)
                self.last.append(key)
            counts[who] += 1
            self.reads[key] = (who, counts[who])

    def slot(self, name, n):
        if n not in (self.early if name in EARLY else self.late):
            return None
        if self.setup:
            return PREP_AT[name][0] if n == 0 else SECOND_AT[name]
        return PREP_AT[name][1] + NU * n


def build(nc, x, w_attn, b_attn, w_proj, b_proj, wi, bi, wo, bo, lora_a, lora_b, gate_w, gate_b, out):
    ctx = ExitStack()
    with ctx:
        def sb(name, shape, dt=F32):
            return ctx.enter_context(nc.sbuf_tensor(name, shape, dt))

        def sem(name):
            return ctx.enter_context(nc.semaphore(name))

        ident = sb("ident", [P, P])
        ident16 = sb("ident16", [P, P], BF16)
        ones = sb("ones", [P, T])
        causal = sb("causal", [P, P])
        minus_half = sb("minus_half", [P, NA])
        half_mark = sb("half_mark", [P, 1])
        not_first = sb("not_first", [P, 2])
        rank = sb("rank", [P, NA, NE])
        ar = sb("ar", [P, NA_RING, T])
        raw = ar[:, :, :].rearrange("p n t -> p (n t)")
        raw_attn = raw[:, 0:384].rearrange("p (t c) -> p t c", t=3)
        raw_wi = raw[:, 384:896].rearrange("p (f c) -> p f c", f=NF)
        raw_wo = raw[:, 896:1408]
        raw_b = raw[:, 1408:1920].rearrange("p (f e r) -> p f e r", f=NF, e=NE)
        raw_a = raw[:, 1920:2048]
        raw_wp = raw[:, 2048:2176]
        raw_gate = sb("raw_gate", [NE, C])
        raw_bi = sb("raw_bi", [NF, P])
        raw_bqk = sb("raw_bqk", [2, P])
        bqk_dh = sb("bqk_dh", [2, P])
        bias_row = sb("bias_row", [1, P + NE])
        bias2 = sb("bias2", [1, 2, C])
        bias_rows = sb("bias_rows", [ROWS, 2, NA - 1, C], BF16)
        ones16 = sb("ones16", [ROWS, P], BF16)
        wq = sb("wq", [C, P])
        wk = sb("wk", [C, P])
        wv = sb("wv", [C, P])
        wi_t = sb("wi_t", [C, FF])
        wo_t = sb("wo_t", [P, NF, C])
        b_t = sb("b_t", [NE * R, FF])
        a_t = sb("a_t", [C, NE * R])
        wp_t = sb("wp_t", [P, C])
        gate_t = sb("gate_t", [C, NE])
        bi_col = sb("bi_col", [P, NF])
        bqk_col = sb("bqk_col", [P, 2])
        bias_b = sb("bias_b", [P, P + NE])
        xs = sb("xs", [P, XN, NA, C])
        stats = sb("stats", [P, NA, 6])
        mv = sb("mv", [P, NA, 2])
        minus_mean = sb("minus_mean", [P, NA])
        shift = sb("shift", [P, NA])
        var = sb("var", [P, NA])
        rstd = sb("rstd", [P, NA])
        xn = sb("xn", [P, NA, C])
        xnt = sb("xnt", [C, 2, T])
        qk32 = sb("qk32", [P, 2, T])
        parts = sb("parts", [P, 2, 3, T], BF16)
        qs = sb("qs", [ROWS, 2, NH, T], BF16)
        ks = sb("ks", [ROWS, 2, NH, T], BF16)
        va = sb("va", [P, 2, NA, (NH - 1) * VW + OW])
        s0 = sb("s0", [P, FOFF[NA]])
        ft = sb("ft", [P, FOFF[NA]])
        nf = sb("nf", [P, OFF[NA]])
        work = sb("work", [P, NA, WIDE])
        junk = sb("junk", [P, 2, T], BF16)
        greatest = sb("greatest", [P, NA])
        halves = sb("halves", [P, HALVINGS, NA])
        cut = sb("cut", [P, NA])
        above = sb("above", [P, NA])
        step_to = sb("step_to", [P, NA])
        count = sb("count", [P, NA])
        bad = sb("bad", [P, 2, NA])
        flag = sb("flag", [1, 1])
        flag_i = sb("flag_i", [1, 1], mybir.dt.int32)
        pads01 = sb("pads01", [P, NA, PADS])
        query = sb("query", [P, NA])
        reach = sb("reach", [P, NA])
        all_low = sb("all_low", [P, NA])
        few = sb("few", [P, NA])
        pad_no = sb("pad_no", [P, NA, PADS])
        top8 = sb("top8", [P, NA, 8])
        mask = sb("mask", [P, 2, OFF[NA]])
        logit = sb("logit", [P, NA, NE])
        less = sb("less", [P, NA, NE + 1])
        expd = sb("expd", [P, NA, NE + 1])
        eq = sb("eq", [P, NA, NE])
        tie = sb("tie", [P, NA, NE])
        hot = sb("hot", [P, 2, NA, NE])
        best = sb("best", [P, 4, NA])
        den = sb("den", [P, NA])
        vsum = sb("vsum", [P, 2, NA])
        rest = sb("rest", [P, 2, T])
        hot_x = sb("hot_x", [P, 2, 2, NA, NE * R], BF16)
        z = sb("z", [P, T])
        zm = sb("zm", [P, 2, T])
        h = sb("h", [P, 4, T])
        hsum = sb("hsum", [P, NF, T])
        bias_part = hsum[0:1, 0:3, :].rearrange("o f t -> o (f t)").bitcast(BF16)[:, 0:6 * (NA - 1) * C]\
            .rearrange("o (j q a c) -> o j q a c", j=2, q=3, a=NA - 1)
        down = sb("down", [P, NA, C])
        mx = sb("mx", [P, NA_RING, 4])
        pr = sb("pr", [P, NP_RING, T])
        rec = sb("rec", [P, NH])
        y = sb("y", [P, NA, NH, HD])
        yt = sb("yt", [P, NA, P])
        res = sb("res", [P, NA, C])

        def bank(name):
            return ctx.enter_context(nc.psum_tensor(name, [P, 512], F32))

        ps_s = [bank(f"ps_s{i}") for i in range(NS_RING)]
        ps_t = [bank(f"ps_t{i}") for i in range(NT_RING)]
        ps_o = bank("ps_o")
        ps_m = [bank(f"ps_m{i}") for i in range(NM_RING)]

        names = ["w_in", "x_in", "const", "w_prep", "scored", "masked", "shifted", "turned", "weighed",
                 "summed", "normed", "m_full", "act_read", "dve_read", "varred", "rooted", "xn_done",
                 "limited", "ruled", "centred", "split", "stacked", "less_done", "exp_done",
                 "hot_wide", "scanned", "nf_done", "halved", "counted", "rested", "parted", "again",
                 "selected", "mask_done", "h_sum", "stored", "dve_chain", "pool_chain",
                 "act_chain", "sel", "zeroed", "zeroed_1", "w_first", "w_rows"]
        s = {n: sem(n) for n in names}
        w_in, x_in, const, w_prep = s["w_in"], s["x_in"], s["const"], s["w_prep"]
        scored, masked, shifted, turned = s["scored"], s["masked"], s["shifted"], s["turned"]
        weighed, summed, normed = s["weighed"], s["summed"], s["normed"]
        m_full, act_read, dve_read = s["m_full"], s["act_read"], s["dve_read"]
        varred, rooted, xn_done, split, stacked = s["varred"], s["rooted"], s["xn_done"], s["split"], s["stacked"]
        less_done, exp_done, hot_wide = s["less_done"], s["exp_done"], s["hot_wide"]
        scanned, nf_done, selected, mask_done = s["scanned"], s["nf_done"], s["selected"], s["mask_done"]
        h_sum, stored = s["h_sum"], s["stored"]
        dve_chain, pool_chain, act_chain, sel = s["dve_chain"], s["pool_chain"], s["act_chain"], s["sel"]
        zeroed, halved, counted, rested, parted = s["zeroed"], s["halved"], s["counted"], s["rested"], s["parted"]
        zeroed_1, w_first, w_rows = s["zeroed_1"], s["w_first"], s["w_rows"]
        again, limited, ruled, centred = s["again"], s["limited"], s["ruled"], s["centred"]

        x_d = x.rearrange("b (a p) c -> b p a c", p=P)
        out_d = out.rearrange("b (a p) c -> b p a c", p=P)

        def run_block(i, steps, preps, setup=False):
            plan = Plan(steps, preps, setup)
            into = (lambda n: n % 2) if setup else (lambda n: (n + 1) % 2)
            x_into = (lambda n: n % XN) if setup else (lambda n: (n + 1) % XN)
            at = plan.slot
            nth = (lambda n: n) if setup else (lambda n: n - 1)
            end = NU * max(steps, 1) + TAIL

            def full(name, k):
                return plan.number[name, k] + 1

            def wait_full(eng, name, k):
                eng.wait_ge(m_full, full(name, k))

            def wait_read(eng, name, k):
                who, n = plan.reads[name, k]
                eng.wait_ge(act_read if who == "act" else dve_read, n)

            def m_bank(name, k):
                return ps_m[plan.place[name, k] % NM_RING]

            with nc.Block() as block:

                def store(sp, k, part):
                    wait_read(sp, ("proj0", "proj1")[part], k)
                    lo, hi = ((0, NA - 1), (NA - 1, NA))[part]
                    b = i * STEPS + k
                    sp.dma_start(out_d[bass.ds(b, 1), :, lo:hi, :].rearrange("o p a c -> p (o a) c"),
                                 res[:, lo:hi, :]).then_inc(stored, 16)

                @block.sync
                def _(sp):
                    if setup:
                        sp.dma_start(xs[:, 0, :, :], x_d[0]).then_inc(x_in, 16)
                        sp.dma_start(raw_attn, w_attn.rearrange("(t p) c -> p t c", p=P)).then_inc(w_first, 16)
                        sp.dma_start(raw_bqk[:, :], b_attn[0:2 * P].rearrange("(t p) -> t p", p=P)).then_inc(w_first, 16)
                        sp.dma_start(raw_wi, wi.rearrange("(f p) c -> p f c", p=P)).then_inc(w_in, 16)
                        sp.dma_start(raw_wo, wo).then_inc(w_in, 16)
                        for f in range(NF):
                            sp.dma_start(raw_b[:, f], lora_b[:, P * f:P * f + P, :].rearrange("e p r -> p e r"))\
                                .then_inc(w_in, 16)
                        sp.dma_start(raw_a, lora_a.rearrange("e r c -> (e r) c")).then_inc(w_in, 16)
                        sp.dma_start(raw_wp, w_proj).then_inc(w_in, 16)
                        sp.dma_start(raw_gate[:, :], gate_w).then_inc(w_in, 16)
                        sp.dma_start(raw_bi[:, :], bi.rearrange("(f p) -> f p", p=P)).then_inc(w_in, 16)
                        sp.dma_start(bias_row[:, 0:P], b_attn[2 * P:3 * P].rearrange("(o p) -> o p", o=1))\
                            .then_inc(w_in, 16)
                        sp.dma_start(bias_row[:, P:P + NE], gate_b.rearrange("(o p) -> o p", o=1)).then_inc(w_in, 16)
                        sp.dma_start(bias2[:, 0, :], b_proj.rearrange("(o p) -> o p", o=1)).then_inc(w_in, 16)
                        sp.dma_start(bias2[:, 1, :], bo.rearrange("(o p) -> o p", o=1)).then_inc(w_in, 16)
                    def fetch(n):
                        if nth(n) >= 1:
                            sp.wait_ge(x_in, 16 * nth(n))
                        if n >= XN - 1:
                            wait_read(sp, "down1", n - (XN - 1))
                        if setup:
                            b = n
                        elif n + 1 < STEPS:
                            b = i * STEPS + (n + 1)
                        else:
                            b = (n + 1 - STEPS) + (B - STEPS) - i * (B - STEPS)
                        sp.dma_start(xs[:, x_into(n), :, :],
                                     x_d[bass.ds(b, 1)].rearrange("o p a c -> p (o a) c")).then_inc(x_in, 16)

                    def make_stacks(n):
                        if not setup:
                            sp.wait_ge(scored, NU * n)
                        for t in range(2):
                            if setup:
                                sp.wait_ge((zeroed, zeroed_1)[n], 2)
                            sp.wait_ge(split, 2 * nth(n) + t + 1)
                            stack, part = ((qs, Q_PART), (ks, K_PART))[t]
                            for j in range(len(part)):
                                sp.dma_start(stack[8 * j:8 * j + 8, into(n), :, :], parts[:, t, part[j], :])\
                                    .then_inc(stacked, 16)

                    fetch(1)
                    if setup:
                        make_stacks(0)
                        sp.wait_ge(w_prep, 3)
                        for j in range(2):
                            sp.dma_start(bias_rows[0:3, j, :, :], bias_part[:, j, :, :, :]).then_inc(w_rows, 16)
                        sp.wait_ge(w_rows, 32)
                    for k in range(steps):
                        if k >= 1:
                            make_stacks(k)
                            store(sp, k - 1, 1)
                        if k + 2 <= preps:
                            fetch(k + 2)
                        store(sp, k, 0)
                    make_stacks(preps)
                    if steps:
                        store(sp, steps - 1, 1)
                        sp.wait_ge(stored, 32 * steps)
                    sp.wait_ge(stacked, 192 * len(plan.early))

                @block.gpsimd
                def _(pool):
                    chain = [0]

                    def link(ins):
                        chain[0] += 1
                        ins.then_inc(pool_chain, 1)
                        pool.wait_ge(pool_chain, chain[0])

                    if setup:
                        link(nc.gpsimd.memset(ident[:, :], 0.0))
                        nc.gpsimd.affine_select(out=ident[:, :], in_=ident[:, :], compare_op=ALU.not_equal, fill=1.0,
                                                base=0, pattern=[[-1, P]], channel_multiplier=1).then_inc(const, 1)
                        link(nc.gpsimd.memset(minus_half[:, :], -0.5))
                        link(nc.gpsimd.memset(half_mark[:, :], -MARK / 2))
                        link(nc.gpsimd.memset(not_first[:, :], 1.0))
                        link(nc.gpsimd.affine_select(out=not_first[:, 0:1], in_=not_first[:, 0:1],
                                                     compare_op=ALU.is_gt, fill=0.0, base=0, pattern=[[0, 1]],
                                                     channel_multiplier=1))
                        link(nc.gpsimd.memset(ident16[:, :], 0.0))
                        link(nc.gpsimd.affine_select(out=ident16[:, :], in_=ident16[:, :], compare_op=ALU.not_equal,
                                                     fill=1.0, base=0, pattern=[[-1, P]], channel_multiplier=1))
                        link(nc.gpsimd.memset(causal[:, :], 0.0))
                        link(nc.gpsimd.affine_select(out=causal[:, :], in_=causal[:, :], compare_op=ALU.is_ge,
                                                     fill=-BIG, base=0, pattern=[[-1, P]], channel_multiplier=1))
                        link(nc.gpsimd.iota(query[:, :], pattern=[[P, NA]], base=1, channel_multiplier=1,
                                            allow_small_or_imprecise_dtypes=True))
                        link(nc.gpsimd.iota(pad_no[:, :, :], pattern=[[0, NA], [1, PADS]], base=0, channel_multiplier=0,
                                            allow_small_or_imprecise_dtypes=True))
                        nc.gpsimd.memset(va[:, :, :, :], 1.0).then_inc(const, 1)

                    def pool_prepares(n, t):
                        if setup and n == 0 and t == at("third_k", 0) + 1:
                            for stack in (qs, ks):
                                nc.gpsimd.memset(stack[:, 1].rearrange("p h t -> p (h t)").bitcast(F32), 0.0)\
                                    .then_inc(zeroed_1, 1)
                        if t == at("root", n):
                            pool.wait_ge(varred, nth(n) + 1)
                            if setup:
                                pool.wait_ge(pool_chain, chain[0])
                            nc.gpsimd.tensor_tensor(rstd[:, :], var[:, :], minus_half[:, :], ALU.pow).then_inc(rooted, 1)
                            pool.wait_ge(rooted, nth(n) + 1)
                            nc.gpsimd.tensor_tensor(shift[:, :], minus_mean[:, :], rstd[:, :], ALU.mult).then_inc(centred, 1)
                        for j in range(2):
                            if t == at(("rest_q", "rest_k")[j], n):
                                wait_read(pool, ("q", "k")[j], n)
                                nc.gpsimd.tensor_tensor(rest[:, j, :], qk32[:, j, :], parts[:, j, 0, :], ALU.subtract)\
                                    .then_inc(rested, 1)
                            if t == at(("third_q", "third_k")[j], n):
                                pool.wait_ge(parted, 2 * nth(n) + j + 1)
                                nc.gpsimd.tensor_tensor(parts[:, j, 2, :], rest[:, j, :], parts[:, j, 1, :],
                                                        ALU.subtract).then_inc(split, 1)
                        for a in range(NA):
                            if t == at(f"s{a}", n):
                                wait_read(pool, f"s{a}", n)
                                edge = s0[:, FOFF[a]:FOFF[a] + P]
                                nc.gpsimd.affine_select(out=edge, in_=edge, compare_op=ALU.is_gt, fill=0.0, base=0,
                                                        pattern=[[1, P]], channel_multiplier=-1).then_inc(ruled, 1)
                            if t == at(f"f{a}", n):
                                wait_read(pool, f"f{a}", n)
                                edge = nf[:, OFF[a] + P * a:OFF[a + 1]]
                                nc.gpsimd.tensor_tensor(edge, edge, causal[:, :], ALU.add).then_inc(nf_done, 1)
                            if t != at(f"mask_{a}", n):
                                continue
                            pool.wait_ge(limited, NA * n + a + 1)
                            edge = work[:, a, PADS + P * a:PADS + P * a + P]
                            link(nc.gpsimd.affine_select(out=edge, in_=edge, compare_op=ALU.not_equal, fill=0.0,
                                                         base=0, pattern=[[-1, P]], channel_multiplier=1))
                            if not setup:
                                pool.wait_ge(masked, NH * NA * n)
                            nc.gpsimd.tensor_tensor(mask[:, into(n), OFF[a]:OFF[a + 1]], nf[:, OFF[a]:OFF[a + 1]],
                                                    work[:, a, PADS:PADS + P * (a + 1)], ALU.subtract)\
                                .then_inc(mask_done, 1)

                    for t in range(end):
                        k, o = divmod(t, NU)
                        if k < steps:
                            a, h0, g = UNITS[o]
                            w = P * (a + 1)
                            for j in range(g):
                                col = ar[:, t % NA_RING, w * j:w * j + w]
                                pool.wait_ge(masked, NH * NA * k + HEADS_TO[o] - g + j + 1)
                                nc.gpsimd.tensor_scalar(col, col, -1.0, mx[:, t % NA_RING, j:j + 1], ALU.mult, ALU.add)\
                                    .then_inc(shifted, 1)
                        for n in range(preps + 1):
                            pool_prepares(n, t)
                        if k < steps:
                            for f in range(NF):
                                if o == dict((n, q) for n, q, _ in FFN_JOBS)[f"h{f}1"] + 1:
                                    wait_read(pool, f"h{f}1", k)
                                    if f == 0 and k >= 1:
                                        wait_full(pool, "down1", k - 1)
                                    nc.gpsimd.tensor_tensor(hsum[:, f, :], h[:, 2 * (f % 2), :], h[:, 2 * (f % 2) + 1, :],
                                                            ALU.add).then_inc(h_sum, 1)

                @block.scalar
                def _(act):
                    chain = [0]

                    def link(ins):
                        chain[0] += 1
                        ins.then_inc(act_chain, 1)

                    def copy(dst, src, name, k, last=True, **kw):
                        ins = nc.scalar.activation(dst, src, ACT.Identity, **kw)
                        ins.then_inc(act_read if last else act_chain, 1)

                    def weights(name):
                        m = m_bank(name, 0)
                        if name == "w_attn":
                            copy(wq[:, :].rearrange("c (d h) -> c d h", d=HD),
                                 m[:, 0:128].rearrange("c (h d) -> c d h", d=HD), name, 0, False)
                            copy(wk[:, :].rearrange("c (d h) -> c d h", d=HD),
                                 m[:, 128:256].rearrange("c (h d) -> c d h", d=HD), name, 0, False)
                            copy(wv[:, :], m[:, 256:384], name, 0, False)
                            copy(bqk_col[:, 0:1], m[:, 384:385], name, 0, False, scale=SCALE)
                            copy(bqk_col[:, 1:2], m[:, 385:386], name, 0)
                        elif name == "w_in":
                            copy(wi_t[:, :], m[:, :], name, 0)
                        elif name == "w_out":
                            copy(wo_t[:, :, :].rearrange("p f c -> p (f c)"), m[:, :], name, 0)
                        elif name == "lora_b":
                            copy(b_t[:, :], m[:, :], name, 0)
                        elif name == "small":
                            copy(a_t[:, :], m[:, 0:128], name, 0, False)
                            copy(wp_t[:, :], m[:, 128:256], name, 0, False)
                            copy(gate_t[:, :], m[:, 256:264], name, 0, False)
                            copy(bi_col[:, :], m[:, 264:268], name, 0)
                        elif name == "rows":
                            copy(bias_b[:, :], m[:, 0:P + NE], name, 0)

                    def act_prepares(n, t):
                        if t == at("norm", n):
                            act.wait_ge(centred, nth(n) + 1)
                            if nth(n) >= 1:
                                wait_full(act, "xt", n - 1)
                            for a in range(NA):
                                nc.scalar.activation(xn[:, a, :], xs[:, x_into(n), a, :], ACT.Identity,
                                                     scale=rstd[:, a:a + 1], bias=shift[:, a:a + 1]).then_inc(xn_done, 1)
                        if t == at("choices", n):
                            act.wait_ge(less_done, nth(n) + 1)
                            nc.scalar.activation(expd[:, :, :], less[:, :, :], ACT.Exp).then_inc(exp_done, 1)
                            if n >= 1 and not setup:
                                wait_full(act, "mask1", n - 1)
                            for j in range(2):
                                nc.scalar.activation(
                                    hot_x[:, into(n), j].rearrange("p a (e r) -> p (a e) r", r=R),
                                    hot[:, j].rearrange("p a (e o) -> p (a e) o", o=1).to_broadcast([P, NA * NE, R]),
                                    ACT.Identity).then_inc(hot_wide, 1)
                        for j in range(2):
                            if t == at(("second_q", "second_k")[j], n):
                                act.wait_ge(rested, 2 * nth(n) + j + 1)
                                nc.scalar.activation(parts[:, j, 1, :], rest[:, j, :], ACT.Identity).then_inc(parted, 1)
                        for a in range(NA):
                            if t == at(f"mask_{a}", n):
                                act.wait_ge(selected, n + 1)
                                data = work[:, a, PADS:PADS + P * (a + 1)]
                                nc.scalar.activation(data, data, ACT.Relu, bias=half_mark[:, :])\
                                    .then_inc(limited, 1)
                        r, odd = divmod(t - at("search", n), 2) if n in plan.late else (-1, 0)
                        if 0 <= r < HALVINGS and not odd:
                            act.wait_ge(halved, (HALVINGS + 1) * n + r + 1)
                            if r == 0:
                                act.wait_ge(nf_done, NA * (n + 1))
                            for a in (2, 3):
                                nc.scalar.activation(junk[:, a - 2, 0:P * (a + 1)], nf[:, OFF[a]:OFF[a + 1]], ACT.Sign,
                                                     bias=cut[:, a:a + 1], scale=-1.0, accum_out=above[:, a:a + 1])\
                                    .then_inc(counted, 1)

                    for t in range(end):
                        k, o = divmod(t, NU)
                        for name, n in plan.at.get(t, []):
                            if plan.reads[name, n][0] != "act":
                                continue
                            wait_full(act, name, n)
                            m = m_bank(name, n)
                            if name in dict(SETUP_JOBS):
                                weights(name)
                            elif name == "xt":
                                if n >= 1 and not setup:
                                    wait_full(act, f"h{NF - 1}1", n - 1)
                                copy(xnt[:, into(n), :], m[:, :], name, n)
                            elif name in ("q", "k"):
                                j = ("q", "k").index(name)
                                if nth(n) >= 1:
                                    act.wait_ge(split, 2 * nth(n))
                                    act.wait_ge(stacked, 192 * nth(n))
                                if setup:
                                    wait_read(act, "w_attn", 0)
                                copy(qk32[:, j, :], m[:, :], name, n, False, bias=bqk_col[:, j:j + 1],
                                     scale=(SCALE, 1.0)[j])
                                copy(parts[:, j, 0, :], m[:, :], name, n, bias=bqk_col[:, j:j + 1],
                                     scale=(SCALE, 1.0)[j])
                            elif name[0] == "s":
                                j = int(name[1])
                                if n >= 1:
                                    act.wait_ge(scanned, NA * (n - 1) + j + 1)
                                if setup:
                                    act.wait_ge(const, 2)
                                w = T - P * j
                                nc.scalar.activation(s0[:, FOFF[j]:FOFF[j] + w], m[:, 0:w], ACT.Relu,
                                                     scale=not_first[:, min(j, 1):min(j, 1) + 1]).then_inc(act_read, 1)
                            elif name == "z":
                                if n >= 1:
                                    wait_read(act, "mask1", n - 1)
                                copy(z[:, :], m[:, :], name, n)
                            elif name[0] == "h":
                                f, j = int(name[1]), int(name[2])
                                if NF * n + f >= 2:
                                    act.wait_ge(h_sum, NF * n + f - 1)
                                nc.scalar.activation(h[:, 2 * (f % 2) + j, :], m[:, :], ACT.Relu, bias=bi_col[:, f:f + 1])\
                                    .then_inc(act_read, 1)
                            elif name[0:2] == "yt":
                                a = int(name[2])
                                if n >= 1 and a in (0, 3):
                                    wait_full(act, ("proj0", "proj1")[a == 3], n - 1)
                                copy(yt[:, a, :], m[:, 0:P], name, n)
                        u = t - LAG_T
                        if 0 <= u < NU * steps:
                            a, h0, g = UNITS[u % NU]
                            act.wait_ge(turned, u + 1)
                            if u >= NP_RING:
                                act.wait_ge(summed, u - NP_RING + 1)
                            w = P * (a + 1) * g
                            nc.scalar.activation(pr[:, u % NP_RING, 0:w], ps_t[u % NT_RING][:, 0:w], ACT.Exp, scale=-1.0)\
                                .then_inc(weighed, 1)
                        for n in range(preps + 1):
                            act_prepares(n, t)

                @block.tensor
                def _(pe):
                    def fill(name, n):
                        i_place = plan.place[name, n]
                        if i_place >= NM_RING:
                            wait_read(pe, *plan.last[i_place - NM_RING])
                        m = m_bank(name, n)
                        c = into(n)
                        if name == "w_attn":
                            pe.wait_ge(w_first, 32)
                            pe.wait_ge(const, 1)
                            for j in range(3):
                                nc.tensor.transpose(m[:, P * j:P * j + P], raw_attn[:, j, :], ident[:, :])
                            pe.wait_ge(w_prep, 1)
                            last = nc.tensor.transpose(m[:, 384:386], bqk_dh[:, :], ident[0:2, 0:2])
                        elif name == "w_in":
                            for f in range(NF):
                                last = nc.tensor.transpose(m[:, P * f:P * f + P], raw_wi[:, f, :], ident[:, :])
                        elif name == "w_out":
                            for f in range(NF):
                                last = nc.tensor.transpose(m[:, P * f:P * f + P], raw_wo[:, P * f:P * f + P], ident[:, :])
                        elif name == "lora_b":
                            for f in range(NF):
                                last = nc.tensor.transpose(m[:, P * f:P * f + P],
                                                           raw_b[:, f].rearrange("p e r -> p (e r)"), ident[:, :])
                        elif name == "small":
                            pe.wait_ge(w_in, 16 * NW)
                            nc.tensor.transpose(m[:, 0:P], raw_a, ident[:, :])
                            nc.tensor.transpose(m[:, P:2 * P], raw_wp, ident[:, :])
                            nc.tensor.transpose(m[:, 256:264], raw_gate[:, :], ident[0:NE, 0:NE])
                            last = nc.tensor.transpose(m[:, 264:268], raw_bi[:, :], ident[0:NF, 0:NF])
                        elif name == "rows":
                            pe.wait_ge(w_prep, 2)
                            last = nc.tensor.matmul(m[:, 0:P + NE], ones[0:1, 0:P], bias_row[:, :], start=True, stop=True)
                        elif name == "xt":
                            pe.wait_ge(xn_done, NA * (nth(n) + 1))
                            for a in range(NA):
                                last = nc.tensor.transpose(m[:, P * a:P * a + P], xn[:, a, :], ident[:, :])
                        elif name in ("q", "k"):
                            wait_read(pe, "xt", n)
                            last = nc.tensor.matmul(m[:, :], (wq if name == "q" else wk)[:, :], xnt[:, c, :],
                                                    start=True, stop=True)
                        elif name == "v":
                            for a in range(NA):
                                last = nc.tensor.matmul(m[:, P * a:P * a + P], xnt[:, c, P * a:P * a + P], wv[:, :],
                                                        start=True, stop=True)
                        elif name == "gate":
                            wait_read(pe, "xt", n)
                            if setup:
                                wait_read(pe, "small", 0)
                            for a in range(NA):
                                last = nc.tensor.matmul(m[:, NE * a:NE * a + NE], xnt[:, c, P * a:P * a + P], gate_t[:, :],
                                                        start=True, stop=True)
                        elif name[0] == "s":
                            j = int(name[1])
                            if nth(n) >= 0:
                                pe.wait_ge(stacked, 192 * (nth(n) + 1))
                            last = nc.tensor.matmul(m[:, 0:T - P * j], ks[:, c, 0, P * j:P * j + P], qs[:, c, 0, P * j:T],
                                                    start=True, stop=True)
                        elif name == "flag":
                            pe.wait_ge(sel, n + 1)
                            last = nc.tensor.matmul(m[0:1, 0:NA], ones[:, 0:1], bad[:, 0, :], start=True, stop=True)
                        elif name[0] == "f":
                            a = int(name[1])
                            pe.wait_ge(scanned, NA * n + a + 1)
                            for j in range(a + 1):
                                at = FOFF[j] + P * (a - j)
                                last = nc.tensor.transpose(m[:, P * j:P * j + P], ft[:, at:at + P], ident[:, :])
                        elif name == "z":
                            last = nc.tensor.matmul(m[:, :], a_t[:, :], xnt[:, n % 2, :], start=True, stop=True)
                        elif name[0:4] == "mask":
                            j = int(name[4])
                            for a in range(NA):
                                last = nc.tensor.matmul(m[:, P * a:P * a + P], hot_x[:, n % 2, j, a, :], ident16[:, :],
                                                        start=True, stop=True)
                        elif name[0] == "h":
                            f, j = int(name[1]), int(name[2])
                            wait_read(pe, f"mask{j}", n)
                            if j == 0:
                                nc.tensor.matmul(m[:, :], wi_t[:, P * f:P * f + P], xnt[:, n % 2, :], start=True, stop=False)
                            else:
                                wait_read(pe, f"h{f}0", n)
                            last = nc.tensor.matmul(m[:, :], b_t[:, P * f:P * f + P], zm[:, j, :], start=False, stop=True,
                                                    skip_group_check=(j == 1))
                        elif name[0:4] == "down":
                            pe.wait_ge(h_sum, NF * (n + 1))
                            lo, hi = HALF[int(name[4])][0], HALF[int(name[4])][-1] + 1
                            nc.tensor.matmul(m[:, P * lo:P * hi], ones16[:, :],
                                             bias_rows[:, 1, 0:hi - lo, :].rearrange("p a c -> p (a c)"), start=True, stop=False)
                            for a in range(lo, hi):
                                for f in range(NF):
                                    last = nc.tensor.matmul(m[:, P * a:P * a + P], hsum[:, f, P * a:P * a + P],
                                                            wo_t[:, f, :], start=False, stop=(a == hi - 1 and f == NF - 1))
                        elif name[0:2] == "yt":
                            a = int(name[2])
                            pe.wait_ge(normed, NA * n + a + 1)
                            last = nc.tensor.transpose(m[:, 0:P], y[:, a, :, :].rearrange("p h d -> p (h d)"), ident[:, :])
                        elif name[0:4] == "proj":
                            lo, hi = ((0, NA - 1), (NA - 1, NA))[int(name[4])]
                            wait_read(pe, f"yt{hi - 1}", n)
                            nc.tensor.matmul(m[:, 0:P * (hi - lo)], ones16[:, :],
                                             bias_rows[:, 0, 0:hi - lo, :].rearrange("p a c -> p (a c)"), start=True, stop=False)
                            for a in range(lo, hi):
                                last = nc.tensor.matmul(m[:, P * (a - lo):P * (a - lo) + P], yt[:, a, :], wp_t[:, :],
                                                        start=False, stop=(a == hi - 1))
                        last.then_inc(m_full, 1)

                    def score(u):
                        k, o = divmod(u, NU)
                        a, h0, g = UNITS[o]
                        w = P * (a + 1)
                        if o == 0 and k >= 2:
                            pe.wait_ge(stacked, 192 * (k - 1))
                        if u >= NS_RING:
                            kk, oo = divmod(u - NS_RING, NU)
                            pe.wait_ge(masked, NH * NA * kk + HEADS_TO[oo])
                        for j in range(g):
                            last = nc.tensor.matmul(ps_s[u % NS_RING][:, w * j:w * j + w], qs[:, k % 2, h0 + j, P * a:P * a + P],
                                                    ks[:, k % 2, h0 + j, 0:w], start=True, stop=True)
                        last.then_inc(scored, 1)

                    def turn(u):
                        k, o = divmod(u, NU)
                        a, h0, g = UNITS[o]
                        pe.wait_ge(shifted, NH * NA * k + HEADS_TO[o])
                        if u >= NT_RING:
                            pe.wait_ge(weighed, u - NT_RING + 1)
                        for j in range(g * (a + 1)):
                            last = nc.tensor.transpose(ps_t[u % NT_RING][:, P * j:P * j + P],
                                                       ar[:, u % NA_RING, P * j:P * j + P], ident[:, :])
                        last.then_inc(turned, 1)

                    def weigh(u):
                        k, o = divmod(u, NU)
                        a, h0, g = UNITS[o]
                        pe.wait_ge(weighed, u + 1)
                        if h0 == 0 and NA * k + a >= 1:
                            pe.wait_ge(normed, NA * k + a)
                        for j in range(g):
                            hh = h0 + j
                            for c in range(a + 1):
                                at = P * ((a + 1) * j + c)
                                last = nc.tensor.matmul(ps_o[:, OW * hh:OW * hh + OW], pr[:, u % NP_RING, at:at + P],
                                                        va[:, k % 2, c, VW * hh:VW * hh + OW], start=(c == 0), stop=(c == a))
                        last.then_inc(summed, 1)

                    for t in range(end):
                        for name, n in plan.at.get(t, []):
                            fill(name, n)
                        if t < NU * steps:
                            score(t)
                        if 0 <= t - LAG_T < NU * steps:
                            turn(t - LAG_T)
                        if 0 <= t - LAG_P < NU * steps:
                            weigh(t - LAG_P)

                @block.vector
                def _(dve):
                    chain = [0]

                    def link(ins):
                        chain[0] += 1
                        ins.then_inc(dve_chain, 1)
                        dve.wait_ge(dve_chain, chain[0])

                    def constants():
                        for stack in (qs, ks):
                            nc.vector.memset(stack[:, 0].rearrange("p h t -> p (h t)").bitcast(F32), 0.0)\
                                .then_inc(zeroed, 1)
                        nc.vector.memset(ones[:, :], 1.0).then_inc(w_prep, 1)
                        for e in range(NE):
                            link(nc.vector.memset(rank[:, :, e:e + 1], float(NE - e)))
                        dve.wait_ge(w_in, 16 * NW)
                        link(nc.vector.tensor_scalar(bias2[:, 1, :], bias2[:, 1, :], 2.0, None, ALU.mult))
                        for part in range(3):
                            link(nc.vector.tensor_copy(bias_part[:, :, part, 0, :], bias2[:, :, :]))
                            if part < 2:
                                link(nc.vector.tensor_tensor(bias2[:, :, :], bias2[:, :, :], bias_part[:, :, part, 0, :],
                                                             ALU.subtract))
                        link(nc.vector.memset(bias_rows[:, :, :, :], 0.0))
                        for a in range(1, NA - 1):
                            link(nc.vector.tensor_copy(bias_part[:, :, :, a, :], bias_part[:, :, :, 0, :]))
                        nc.vector.memset(ones16[:, :], 1.0).then_inc(w_prep, 1)
                        dve.wait_ge(const, 2)
                        link(nc.vector.reciprocal(reach[:, :], query[:, :]))
                        link(nc.vector.tensor_scalar(reach[:, :], reach[:, :], REACH * KEEP, 1.0, ALU.mult, ALU.min))
                        link(nc.vector.tensor_scalar(all_low[:, :], query[:, :], KEEP + 0.5, None, ALU.is_lt))
                        for a in range(NA):
                            w = P * (a + 1)
                            link(nc.vector.memset(few[:, a:a + 1], float(w - AIM if a < 2 else w - 2 * AIM)))

                    def moments(n):
                        c = into(n)
                        dve.wait_ge(x_in, 16 * (nth(n) + 1))
                        if nth(n) >= 1:
                            dve.wait_ge(centred, nth(n))
                        for a in range(NA):
                            last = nc.vector.bn_stats(stats[:, a, :], xs[:, x_into(n), a, :])
                            last.then_inc(dve_chain, 1)
                            chain[0] += 1
                        dve.wait_ge(dve_chain, chain[0])
                        for a in range(NA):
                            nc.vector.bn_aggr(mv[:, a, :], stats[:, a, :]).then_inc(dve_chain, 1)
                            chain[0] += 1
                        dve.wait_ge(dve_chain, chain[0])
                        link(nc.vector.tensor_scalar(minus_mean[:, :], mv[:, :, 0], -1.0, None, ALU.mult))
                        nc.vector.tensor_scalar(var[:, :], mv[:, :, 1], EPS, None, ALU.add).then_inc(varred, 1)

                    def wide(col):
                        return col.rearrange("p (a o) -> p a o", o=1).to_broadcast([P, NA, NE])

                    def choose(j):
                        link(nc.vector.tensor_reduce(best[:, j, :], logit[:, :, :], AX, ALU.max))
                        link(nc.vector.tensor_tensor(eq[:, :, :], logit[:, :, :], wide(best[:, j, :]), ALU.is_equal))
                        link(nc.vector.tensor_tensor(tie[:, :, :], eq[:, :, :], rank[:, :, :], ALU.mult))
                        link(nc.vector.tensor_reduce(best[:, 2 + j, :], tie[:, :, :], AX, ALU.max))
                        ins = nc.vector.tensor_tensor(hot[:, j], tie[:, :, :], wide(best[:, 2 + j, :]), ALU.is_equal)
                        return ins

                    def route(n):
                        wait_full(dve, "gate", n)
                        if setup:
                            wait_read(dve, "rows", 0)
                        if nth(n) >= 1:
                            dve.wait_ge(hot_wide, 2 * nth(n))
                        m = m_bank("gate", n)
                        nc.vector.tensor_tensor(
                            logit[:, :, :], m[:, 0:NA * NE].rearrange("p (a e) -> p a e", e=NE),
                            bias_b[:, P:P + NE].rearrange("p (o e) -> p o e", o=1).to_broadcast([P, NA, NE]), ALU.add)\
                            .then_inc(dve_read, 1)
                        dve.wait_ge(dve_read, plan.reads["gate", n][1])
                        link(choose(0))

                    def route_second(n):
                        link(nc.vector.tensor_tensor(less[:, :, 0:NE], logit[:, :, :], wide(best[:, 0, :]), ALU.subtract))
                        link(nc.vector.tensor_scalar(eq[:, :, :], hot[:, 0], -BIG, None, ALU.mult))
                        link(nc.vector.tensor_tensor(logit[:, :, :], logit[:, :, :], eq[:, :, :], ALU.add))
                        link(choose(1))
                        link(nc.vector.tensor_tensor(hot[:, 1], hot[:, 1], hot[:, 0], ALU.subtract))
                        nc.vector.tensor_tensor(less[:, :, NE:NE + 1].rearrange("p a o -> p (a o)"), best[:, 1, :],
                                                best[:, 0, :], ALU.subtract).then_inc(less_done, 1)

                    def share(n):
                        dve.wait_ge(exp_done, nth(n) + 1)
                        link(nc.vector.tensor_reduce(den[:, :], expd[:, :, 0:NE], AX, ALU.add))
                        link(nc.vector.reciprocal(den[:, :], den[:, :]))
                        c = into(n)
                        link(nc.vector.tensor_scalar(vsum[:, c, :], expd[:, :, NE:NE + 1].rearrange("p a o -> p (a o)"),
                                                     1.0, None, ALU.add))
                        link(nc.vector.tensor_tensor(vsum[:, c, :], vsum[:, c, :], den[:, :], ALU.mult))

                    def forget(n, j):
                        if j == 0 and n >= 1:
                            wait_full(dve, f"f{NA - 1}", n - 1)
                        w = T - P * j
                        link(nc.vector.memset(ft[:, FOFF[j]:FOFF[j] + 1], 0.0))
                        dve.wait_ge(ruled, NA * n + j + 1)
                        nc.vector.tensor_tensor_scan(ft[:, FOFF[j] + 1:FOFF[j] + w], ones[:, 0:w - 1],
                                                     s0[:, FOFF[j]:FOFF[j] + w - 1], 0.0, ALU.mult, ALU.add)\
                            .then_inc(scanned, 1)

                    def search_start(n):
                        dve.wait_ge(dve_read, plan.reads[f"f{NA - 1}", n][1])
                        link(nc.vector.tensor_tensor(step_to[:, :], greatest[:, :], reach[:, :], ALU.mult))
                        for r in range(HALVINGS):
                            chain[0] += 1
                            nc.vector.tensor_scalar(halves[:, r, :], step_to[:, :], 0.5 ** (r + 1), None, ALU.mult)\
                                .then_inc(dve_chain, 1)
                        dve.wait_ge(dve_chain, chain[0])
                        nc.vector.tensor_copy(cut[:, :], halves[:, 0, :]).then_inc(halved, 1)

                    def search_count(n, r):
                        dve.wait_ge(halved, (HALVINGS + 1) * n + r + 1)
                        if r == 0:
                            dve.wait_ge(nf_done, NA * (n + 1))
                            if n >= 1:
                                dve.wait_ge(mask_done, NA * n)
                        for a in (0, 1):
                            w = P * (a + 1)
                            chain[0] += 1
                            nc.vector.tensor_scalar(work[:, a, PADS:PADS + w], nf[:, OFF[a]:OFF[a + 1]], cut[:, a:a + 1],
                                                    None, ALU.is_lt, ALU.add, accum_out=above[:, a:a + 1])\
                                .then_inc(dve_chain, 1)

                    def search_step(n, r):
                        dve.wait_ge(dve_chain, chain[0])
                        dve.wait_ge(counted, 2 * HALVINGS * n + 2 * (r + 1))
                        link(nc.vector.tensor_tensor(step_to[:, :], above[:, :], few[:, :], ALU.is_ge))
                        link(nc.vector.scalar_tensor_tensor(out=step_to[:, :], in0=step_to[:, :], scalar=-0.5,
                                                            in1=halves[:, r, :], op0=ALU.add, op1=ALU.mult))
                        nc.vector.tensor_tensor(cut[:, :], cut[:, :], step_to[:, :], ALU.add).then_inc(halved, 1)

                    def under_threshold(n, tiles):
                        if 0 in tiles:
                            dve.wait_ge(halved, (HALVINGS + 1) * (n + 1))
                            link(nc.vector.scalar_tensor_tensor(out=cut[:, :], in0=all_low[:, :], scalar=-BIG / 10,
                                                                in1=cut[:, :], op0=ALU.mult, op1=ALU.add))
                        for a in tiles:
                            chain[0] += 1
                            nc.vector.tensor_scalar(work[:, a, PADS:PADS + P * (a + 1)], nf[:, OFF[a]:OFF[a + 1]],
                                                    cut[:, a:a + 1], None, ALU.is_ge, ALU.add,
                                                    accum_out=count[:, a:a + 1]).then_inc(dve_chain, 1)

                    def in_reach():
                        dve.wait_ge(dve_chain, chain[0])
                        link(nc.vector.tensor_scalar(bad[:, 0, :], count[:, :], KEEP + 0.5, None, ALU.is_gt))
                        link(nc.vector.scalar_tensor_tensor(out=bad[:, 1, :], in0=all_low[:, :], scalar=1000.0,
                                                            in1=count[:, :], op0=ALU.mult, op1=ALU.add))
                        link(nc.vector.tensor_scalar(bad[:, 1, :], bad[:, 1, :], KEEP - SLACK - 0.5, None, ALU.is_lt))
                        nc.vector.tensor_tensor(bad[:, 0, :], bad[:, 0, :], bad[:, 1, :], ALU.add).then_inc(sel, 1)
                        link(nc.vector.tensor_scalar(count[:, :], count[:, :], SLACK - KEEP, None, ALU.add))
                        link(nc.vector.tensor_tensor(pads01[:, :, :], pad_no[:, :, :],
                                                     count[:, :].rearrange("p (a o) -> p a o", o=1)
                                                     .to_broadcast([P, NA, PADS]), ALU.is_lt))
                        link(nc.vector.tensor_scalar(work[:, :, 0:PADS], pads01[:, :, :], 3.1e38, MARK, ALU.mult, ALU.add))

                    def marks(tiles):
                        for a in tiles:
                            chain[0] += 1
                            data = work[:, a, PADS:PADS + P * (a + 1)]
                            nc.vector.scalar_tensor_tensor(out=data, in0=data, scalar=MARK, in1=nf[:, OFF[a]:OFF[a + 1]],
                                                           op0=ALU.mult, op1=ALU.add).then_inc(dve_chain, 1)
                        dve.wait_ge(dve_chain, chain[0])

                    def eight_largest(tiles):
                        dve.wait_ge(dve_chain, chain[0])
                        for a in tiles:
                            chain[0] += 1
                            nc.vector.max(top8[:, a, :], work[:, a, 0:PADS + P * (a + 1)]).then_inc(dve_chain, 1)

                    def replace_largest(tiles):
                        dve.wait_ge(dve_chain, chain[0])
                        for a in tiles:
                            chain[0] += 1
                            row = work[:, a, 0:PADS + P * (a + 1)]
                            nc.vector.match_replace(row, top8[:, a, :], row, MARK).then_inc(dve_chain, 1)

                    def rounds_from_scratch(n):
                        wait_full(dve, "flag", n)
                        nc.vector.tensor_reduce(flag[:, :], m_bank("flag", n)[0:1, 0:NA], AX, ALU.add).then_inc(dve_read, 1)
                        dve.wait_ge(dve_read, plan.reads["flag", n][1])
                        dve.wait_ge(dve_chain, chain[0])
                        link(nc.vector.tensor_copy(flag_i[:, :], flag[:, :]))
                        failed = dve.value_load(flag_i[0:1, 0:1])
                        with dve.If(failed > 0):
                            dve.sem_clear(again)
                            nc.vector.memset(work[:, :, 0:PADS], MARK).then_inc(again, 1)
                            dve.wait_ge(again, 1)
                            nc.vector.memset(work[:, :, 0:8 * ROUNDS - KEEP], 1.0e37).then_inc(again, 1)
                            for a in range(NA):
                                nc.vector.tensor_copy(work[:, a, PADS:PADS + P * (a + 1)], nf[:, OFF[a]:OFF[a + 1]])\
                                    .then_inc(again, 1)
                            dve.wait_ge(again, 2 + NA)
                            with dve.Fori(0, ROUNDS):
                                dve.sem_clear(again)
                                for a in range(NA):
                                    nc.vector.max(top8[:, a, :], work[:, a, 0:PADS + P * (a + 1)]).then_inc(again, 1)
                                for a in range(NA):
                                    dve.wait_ge(again, a + 1)
                                    row = work[:, a, 0:PADS + P * (a + 1)]
                                    nc.vector.match_replace(row, top8[:, a, :], row, MARK).then_inc(again, 1)
                                dve.wait_ge(again, 2 * NA)
                        nc.vector.memset(flag[:, :], 0.0).then_inc(selected, 1)

                    if setup:
                        dve.wait_ge(w_first, 32)
                        nc.vector.tensor_copy(bqk_dh[:, :].rearrange("t (d h) -> t d h", d=HD),
                                              raw_bqk[:, :].rearrange("t (h d) -> t d h", d=HD)).then_inc(w_prep, 1)
                    for t in range(end):
                        k, o = divmod(t, NU)
                        for name, n in plan.at.get(t, []):
                            if plan.reads[name, n][0] != "dve":
                                continue
                            m = m_bank(name, n)
                            if name == "v":
                                wait_full(dve, name, n)
                                if setup:
                                    wait_read(dve, "rows", 0)
                                    dve.wait_ge(const, 2)
                                elif n >= 1:
                                    dve.wait_ge(summed, NU * n)
                                for a in range(NA):
                                    ins = nc.vector.tensor_tensor(
                                        va[:, into(n), a, 0:NH * VW].rearrange("p (h d) -> p h d", d=VW)[:, :, 0:HD],
                                        m[:, P * a:P * a + P].rearrange("p (h d) -> p h d", d=HD),
                                        bias_b[:, 0:P].rearrange("p (h d) -> p h d", d=HD), ALU.add)
                                ins.then_inc(dve_read, 1)
                            elif name == "gate":
                                route(n)
                            elif name == "flag":
                                rounds_from_scratch(n)
                            elif name[0] == "f":
                                a = int(name[1])
                                wait_full(dve, name, n)
                                if n >= 1 and a == 0:
                                    dve.wait_ge(mask_done, NA * n)
                                nc.vector.tensor_scalar(nf[:, OFF[a]:OFF[a + 1]], m[:, 0:P * (a + 1)], -1.0, None,
                                                        ALU.mult, ALU.min, accum_out=greatest[:, a:a + 1])\
                                    .then_inc(dve_read, 1)
                            elif name[0:4] == "mask":
                                j = int(name[4])
                                wait_full(dve, name, n)
                                wait_read(dve, "z", n)
                                if n >= 1:
                                    wait_full(dve, f"h{NF - 1}1", n - 1)
                                nc.vector.tensor_tensor(zm[:, j, :], m[:, :], z[:, :], ALU.mult).then_inc(dve_read, 1)
                            elif name[0:4] == "down":
                                wait_full(dve, name, n)
                                for a in HALF[int(name[4])]:
                                    ins = nc.vector.scalar_tensor_tensor(
                                        out=down[:, a, :], in0=m[:, P * a:P * a + P], scalar=vsum[:, n % 2, a:a + 1],
                                        in1=xs[:, n % XN, a, :], op0=ALU.mult, op1=ALU.add)
                                ins.then_inc(dve_read, 1)
                            elif name[0:4] == "proj":
                                lo, hi = ((0, NA - 1), (NA - 1, NA))[int(name[4])]
                                wait_full(dve, name, n)
                                wait_read(dve, "down1", n)
                                if n >= 1:
                                    dve.wait_ge(stored, 32 * n)
                                nc.vector.tensor_tensor(res[:, lo:hi, :].rearrange("p a c -> p (a c)"),
                                                        m[:, 0:P * (hi - lo)],
                                                        down[:, lo:hi, :].rearrange("p a c -> p (a c)"), ALU.add)\
                                    .then_inc(dve_read, 1)
                        if k < steps:
                            a, h0, g = UNITS[o]
                            w = P * (a + 1)
                            dve.wait_ge(scored, t + 1)
                            if t >= NA_RING:
                                dve.wait_ge(turned, t - NA_RING + 1)
                            if h0 == 0 and k >= 1:
                                dve.wait_ge(mask_done, NA * (k - 1) + a + 1)
                            for j in range(g):
                                nc.vector.tensor_tensor_reduce(
                                    out=ar[:, t % NA_RING, w * j:w * j + w], in0=ps_s[t % NS_RING][:, w * j:w * j + w],
                                    in1=mask[:, k % 2, OFF[a]:OFF[a + 1]], scale=1.0, scalar=MARK, op0=ALU.add, op1=ALU.max,
                                    accum_out=mx[:, t % NA_RING, j:j + 1]).then_inc(masked, 1)
                        for kk in range(steps):
                            for a in range(NA):
                                if t == NU * kk + LAST[a] + LAG_P:
                                    dve.wait_ge(summed, NU * kk + LAST[a] + 1)
                                    if kk >= 1:
                                        wait_full(dve, f"yt{a}", kk - 1)
                                    o3 = ps_o[:, :].rearrange("p (h d) -> p h d", d=OW)
                                    link(nc.vector.reciprocal(rec[:, :].rearrange("p (h o) -> p h o", o=1),
                                                              o3[:, :, HD:VW]))
                                    nc.vector.tensor_tensor(
                                        y[:, a, :, :], o3[:, :, 0:HD],
                                        rec[:, :].rearrange("p (h o) -> p h o", o=1).to_broadcast([P, NH, HD]), ALU.mult)\
                                        .then_inc(normed, 1)
                        for n in range(preps + 1):
                            if t == at("moments", n):
                                moments(n)
                                if setup and n == 0:
                                    constants()
                            if t == at("route", n):
                                route_second(n)
                            if t == at("share", n):
                                share(n)
                            for c in range(NA):
                                if t == at(f"scan{c}", n):
                                    forget(n, c)
                            if n not in plan.late:
                                continue
                            if t == at("search", n) - 1:
                                search_start(n)
                            r, odd = divmod(t - at("search", n), 2)
                            if 0 <= r < HALVINGS:
                                (search_step if odd else search_count)(n, r)
                            for width, tiles in (("narrow", (0, 1, 2)), ("wide", (3,))):
                                if t == at(f"under_{width}", n):
                                    under_threshold(n, tiles)
                            if t == at("reach", n):
                                in_reach()
                            for width, tiles in (("narrow", (0, 1, 2)), ("wide", (3,))):
                                if t == at(f"marks_{width}", n):
                                    marks(tiles)
                            for r in range(FAST):
                                for width, tiles in (("narrow", (0, 1)), ("wide", (2, 3))):
                                    if t == at(f"top{r}_{width}", n):
                                        eight_largest(tiles)
                                for width, tiles in (("narrow", (0, 1, 2)), ("wide", (3,))):
                                    if t == at(f"replace{r}_{width}", n):
                                        replace_largest(tiles)

            with nc.Block() as clear:
                @clear.sync
                def _(sp):
                    for one in s.values():
                        sp.sem_clear(one)

        run_block(0, 0, 1, setup=True)
        with nc.Fori(0, B // STEPS) as i:
            run_block(i, STEPS, STEPS)


_INS = ['L0_attn_x', 'L0_attn_w_attn', 'L0_attn_b_attn', 'L0_attn_w_proj', 'L0_attn_b_proj', 'L0_ffn_wi', 'L0_ffn_bi',
        'L0_ffn_wo', 'L0_ffn_bo', 'L0_ffn_lora_A', 'L0_ffn_lora_B', 'L0_ffn_gate_w', 'L0_ffn_gate_b']


def kernel(**inputs):
    import numpy as _np
    import concourse.bacc as _bacc
    from concourse import mybir as _mybir
    from concourse.bass_utils import run_bass_kernel_spmd as _run
    nc = _bacc.Bacc("TRN2", target_bir_lowering=False, num_devices=1)
    arrays, args = {}, []
    for name in _INS:
        a = _np.ascontiguousarray(inputs[name])
        arrays[f"in_{name}"] = a
        args.append(nc.dram_tensor(f"in_{name}", a.shape, _mybir.dt.from_np(a.dtype), kind="ExternalInput").ap())
    out = nc.dram_tensor("out", (8, 512, 128), _mybir.dt.float32, kind="ExternalOutput").ap()
    build(nc, *args, out)
    r = _run(nc, [arrays], core_ids=[0])
    return r.results[0]["out"]
```
